# Optimizing a Trainium2 kernel written in Bass

```python
import numpy as np
import jax
import jax.numpy as jnp

def _softmax(x, axis=-1):
    return jax.nn.softmax(x, axis=axis)

def _gelu(x):
    return jax.nn.gelu(x, approximate=True)

def _silu(x):
    return jax.nn.silu(x)

def _sigmoid(x):
    return jax.nn.sigmoid(x)

def _layernorm(x, axis=-1, eps=1e-05):
    m = jnp.mean(x, axis=axis, keepdims=True)
    v = jnp.var(x, axis=axis, keepdims=True)
    return (x - m) / jnp.sqrt(v + eps)

def _scatter_add(tgt, idx, src, axis=0):
    return tgt.at[idx].add(src)

def _segment_sum(src, seg, n):
    return jax.ops.segment_sum(src, seg, n)
kernel_name = 'mk_gnn_resnorm_d2_gnn_r32_786f76'

def setup_inputs(seed: int=0):
    np.random.seed(seed)
    _w = jnp.asarray

    def _rec_inputs():
        import jax
        import jax.numpy as jnp
        _gk = jax.random.key(seed)
        x = -0.000202 + 1 * jax.random.normal(jax.random.fold_in(_gk, 1), (3125, 160), jnp.float32)
        _s = jax.random.randint(jax.random.fold_in(_gk, 2), (50000,), 0, 3125, jnp.int32)
        _d = jax.random.randint(jax.random.fold_in(_gk, 3), (50000,), 0, 3125, jnp.int32)
        _loop = jnp.arange(3125, dtype=jnp.int32)
        src = jnp.concatenate([_s, _d, _loop])
        dst = jnp.concatenate([_d, _s, _loop])
        _o = jnp.argsort(dst, stable=True)
        src = src[_o]
        dst = dst[_o]
        edge_attr_10 = jax.random.uniform(jax.random.fold_in(_gk, 12), (103125, 10), jnp.float32, 0.0, 1)
        edge_attr_4 = 0.0012443 + 1.0001 * jax.random.normal(jax.random.fold_in(_gk, 13), (103125, 4), jnp.float32)
        edge_attr_64 = 0.000127647 + 1.00004 * jax.random.normal(jax.random.fold_in(_gk, 14), (103125, 64), jnp.float32)
        node_vec1 = jax.random.uniform(jax.random.fold_in(_gk, 15), (3125, 1), jnp.float32, 0.0, 1)
        node_vec1_n2 = jax.random.uniform(jax.random.fold_in(_gk, 16), (3125, 1), jnp.float32, 0.0, 1)
        node_vec1_n3 = jax.random.uniform(jax.random.fold_in(_gk, 17), (3125, 1), jnp.float32, 0.0, 1)
        return (x, src, dst, edge_attr_10, edge_attr_4, edge_attr_64, node_vec1, node_vec1_n2, node_vec1_n3)
    x, src, dst, edge_attr_10, edge_attr_4, edge_attr_64, node_vec1, node_vec1_n2, node_vec1_n3 = _rec_inputs()

    def _L0_gnn_setup():
        import jax, jax.numpy as jnp
        import numpy as np
        N, E = (1250, 20000)
        S_IN, V_IN = (64, 32)
        S_MID, V_MID = (96, 128)
        S_OUT, V_OUT = (96, 32)
        R = 64
        FC_HID = 64
        W_NUMEL = 64 + 64 + 32 + 32 + 32
        NUM_NEIGHBORS = 16.0

        def _inv(d):
            return 1.0 / jnp.sqrt(jnp.float32(d))

        def _forward(node_features, node_attr, edge_attr, edge_scalars, lin1_ws, lin1_wv, fc_w1, fc_w2, sc_ws, sc_wv, lin2_ws, lin2_wv, edge_src, edge_dst):
            n = node_features.shape[0]
            s = node_features[:, :S_IN]
            v = node_features[:, S_IN:].reshape(n, V_IN, 3)
            a = node_attr
            sc_s = s @ sc_ws * a * _inv(S_IN)
            sc_v = jnp.einsum('nci,cd->ndi', v, sc_wv) * a[:, :, None] * _inv(V_IN)
            h_s = s @ lin1_ws * a * _inv(S_IN)
            h_v = jnp.einsum('nci,cd->ndi', v, lin1_wv) * a[:, :, None] * _inv(V_IN)
            hid = jax.nn.silu(edge_scalars @ fc_w1 * _inv(R))
            w = hid @ fc_w2 * _inv(FC_HID)
            w1, w2, w3, w4, w5 = jnp.split(w, [64, 128, 160, 192], axis=-1)
            es = h_s[edge_src]
            ev = h_v[edge_src]
            e0 = edge_attr[:, :1]
            e1 = edge_attr[:, 1:4]
            m_s1 = w1 * es * e0
            m_s2 = w4 * jnp.einsum('eci,ei->ec', ev, e1) * _inv(3)
            m_v1 = (w2 * es)[:, :, None] * e1[:, None, :]
            m_v2 = w3[:, :, None] * ev * e0[:, :, None]
            m_v3 = w5[:, :, None] * jnp.cross(ev, e1[:, None, :]) * _inv(2)
            mid_s = jnp.concatenate([m_s1, m_s2], axis=-1)
            mid_v = jnp.concatenate([m_v1, m_v2, m_v3], axis=1)
            inv_nn = 1.0 / jnp.sqrt(jnp.float32(NUM_NEIGHBORS))
            agg_s = jax.ops.segment_sum(mid_s, edge_dst, num_segments=n) * inv_nn
            agg_v = jax.ops.segment_sum(mid_v, edge_dst, num_segments=n) * inv_nn
            o_s = agg_s @ lin2_ws * a * _inv(S_MID)
            o_v = jnp.einsum('nci,cd->ndi', agg_v, lin2_wv) * a[:, :, None] * _inv(V_MID)
            pre_s = sc_s + o_s
            pre_v = sc_v + o_v
            scalars = jax.nn.silu(pre_s[:, :64])
            gates = jax.nn.sigmoid(pre_s[:, 64:96])
            gated = gates[:, :, None] * pre_v
            return jnp.concatenate([scalars, gated.reshape(n, 3 * V_OUT)], axis=-1)
        key = jax.random.key(seed)
        ks = jax.random.split(key, 13)
        return {'node_features': jax.random.normal(ks[0], (N, S_IN + 3 * V_IN), jnp.float32), 'node_attr': jnp.ones((N, 1), jnp.float32), 'edge_src': jax.random.randint(ks[1], (E,), 0, N), 'edge_dst': jax.random.randint(ks[2], (E,), 0, N), 'edge_attr': jax.random.normal(ks[3], (E, 4), jnp.float32), 'edge_scalars': jax.random.normal(ks[4], (E, R), jnp.float32), 'lin1_ws': jax.random.normal(ks[5], (S_IN, S_IN), jnp.float32), 'lin1_wv': jax.random.normal(ks[6], (V_IN, V_IN), jnp.float32), 'fc_w1': jax.random.normal(ks[7], (R, FC_HID), jnp.float32), 'fc_w2': jax.random.normal(ks[8], (FC_HID, W_NUMEL), jnp.float32), 'sc_ws': jax.random.normal(ks[9], (S_IN, S_OUT), jnp.float32), 'sc_wv': jax.random.normal(ks[10], (V_IN, V_OUT), jnp.float32), 'lin2_ws': jax.random.normal(ks[11], (S_MID, S_OUT), jnp.float32), 'lin2_wv': jax.random.normal(ks[12], (V_MID, V_OUT), jnp.float32)}
    _L0_gnn_all = _L0_gnn_setup()
    _L0_gnn_in = {k: v for k, v in _L0_gnn_all.items() if k in ('lin1_ws', 'lin1_wv', 'fc_w1', 'fc_w2', 'sc_ws', 'sc_wv', 'lin2_ws', 'lin2_wv')}
    del _L0_gnn_all

    def _L1_gnn_setup():
        import jax, jax.numpy as jnp
        import numpy as np
        N = 25000
        E = 12500
        S = 64
        V = 32
        NB = 10
        H = 100
        WN = 192
        MID = 96
        NUM_NEIGHBORS = 16.0
        C_S = float(np.sin(np.pi / 8.0))
        C_X = float(np.cos(np.pi / 8.0))
        SQRT3 = float(np.sqrt(3.0))

        def fctp_scalar_attr(xs, xv, attr, Ws, Wv):
            s = xs * attr @ Ws
            v = jnp.einsum('nuc,uo->noc', xv * attr[:, :, None], Wv)
            return (s, v)
        key = jax.random.key(seed)
        k = jax.random.split(key, 24)

        def w(i, shape):
            return jax.random.normal(k[i], shape, jnp.float32) / np.sqrt(float(shape[0]))
        return {'node_input': jax.random.normal(k[0], (N, S + 3 * V), jnp.float32), 'node_attr': jax.random.normal(k[1], (N, 1), jnp.float32), 'node_crystal_attr': jax.random.normal(k[2], (N, 1), jnp.float32), 'sym_mask': jax.random.normal(k[3], (N, 1), jnp.float32), 'edge_attr': jax.random.normal(k[4], (E, 4), jnp.float32), 'edge_length_embedded': jax.random.uniform(k[5], (E, NB), dtype=jnp.float32), 'edge_src': jax.random.randint(k[6], (E,), 0, N), 'edge_dst': jax.random.randint(k[7], (E,), 0, N), 'Ws_sc_a': w(8, (S, S)), 'Wv_sc_a': w(9, (V, V)), 'Ws_sc_c': w(10, (S, S)), 'Wv_sc_c': w(11, (V, V)), 'Ws_l1_a': w(12, (S, S)), 'Wv_l1_a': w(13, (V, V)), 'Ws_l1_c': w(14, (S, S)), 'Wv_l1_c': w(15, (V, V)), 'W_fc1': w(16, (NB, H)), 'W_fc2': w(17, (H, WN)), 'Ws_l2_a': w(18, (MID, MID)), 'Wv_l2_a': w(19, (MID, MID)), 'Ws_l2_c': w(20, (MID, MID)), 'Wv_l2_c': w(21, (MID, MID)), 'Ws_l3': w(22, (MID, S)), 'Wv_l3': w(23, (MID, V))}
    _L1_gnn_all = _L1_gnn_setup()
    _L1_gnn_in = {k: v for k, v in _L1_gnn_all.items() if k in ('Ws_sc_a', 'Wv_sc_a', 'Ws_sc_c', 'Wv_sc_c', 'Ws_l1_a', 'Wv_l1_a', 'Ws_l1_c', 'Wv_l1_c', 'W_fc1', 'W_fc2', 'Ws_l2_a', 'Wv_l2_a', 'Ws_l2_c', 'Wv_l2_c', 'Ws_l3', 'Wv_l3')}
    del _L1_gnn_all
    return {'x': x, 'src': src, 'dst': dst, 'edge_attr_10': edge_attr_10, 'edge_attr_4': edge_attr_4, 'edge_attr_64': edge_attr_64, 'node_vec1': node_vec1, 'node_vec1_n2': node_vec1_n2, 'node_vec1_n3': node_vec1_n3, 'L0_gnn_lin1_ws': _L0_gnn_in['lin1_ws'], 'L0_gnn_lin1_wv': _L0_gnn_in['lin1_wv'], 'L0_gnn_fc_w1': _L0_gnn_in['fc_w1'], 'L0_gnn_fc_w2': _L0_gnn_in['fc_w2'], 'L0_gnn_sc_ws': _L0_gnn_in['sc_ws'], 'L0_gnn_sc_wv': _L0_gnn_in['sc_wv'], 'L0_gnn_lin2_ws': _L0_gnn_in['lin2_ws'], 'L0_gnn_lin2_wv': _L0_gnn_in['lin2_wv'], 'L1_gnn_Ws_sc_a': _L1_gnn_in['Ws_sc_a'], 'L1_gnn_Wv_sc_a': _L1_gnn_in['Wv_sc_a'], 'L1_gnn_Ws_sc_c': _L1_gnn_in['Ws_sc_c'], 'L1_gnn_Wv_sc_c': _L1_gnn_in['Wv_sc_c'], 'L1_gnn_Ws_l1_a': _L1_gnn_in['Ws_l1_a'], 'L1_gnn_Wv_l1_a': _L1_gnn_in['Wv_l1_a'], 'L1_gnn_Ws_l1_c': _L1_gnn_in['Ws_l1_c'], 'L1_gnn_Wv_l1_c': _L1_gnn_in['Wv_l1_c'], 'L1_gnn_W_fc1': _L1_gnn_in['W_fc1'], 'L1_gnn_W_fc2': _L1_gnn_in['W_fc2'], 'L1_gnn_Ws_l2_a': _L1_gnn_in['Ws_l2_a'], 'L1_gnn_Wv_l2_a': _L1_gnn_in['Wv_l2_a'], 'L1_gnn_Ws_l2_c': _L1_gnn_in['Ws_l2_c'], 'L1_gnn_Wv_l2_c': _L1_gnn_in['Wv_l2_c'], 'L1_gnn_Ws_l3': _L1_gnn_in['Ws_l3'], 'L1_gnn_Wv_l3': _L1_gnn_in['Wv_l3']}

def reference(x, src, dst, edge_attr_10, edge_attr_4, edge_attr_64, node_vec1, node_vec1_n2, node_vec1_n3, L0_gnn_lin1_ws, L0_gnn_lin1_wv, L0_gnn_fc_w1, L0_gnn_fc_w2, L0_gnn_sc_ws, L0_gnn_sc_wv, L0_gnn_lin2_ws, L0_gnn_lin2_wv, L1_gnn_Ws_sc_a, L1_gnn_Wv_sc_a, L1_gnn_Ws_sc_c, L1_gnn_Wv_sc_c, L1_gnn_Ws_l1_a, L1_gnn_Wv_l1_a, L1_gnn_Ws_l1_c, L1_gnn_Wv_l1_c, L1_gnn_W_fc1, L1_gnn_W_fc2, L1_gnn_Ws_l2_a, L1_gnn_Wv_l2_a, L1_gnn_Ws_l2_c, L1_gnn_Wv_l2_c, L1_gnn_Ws_l3, L1_gnn_Wv_l3):
    import jax
    import jax.numpy as jnp

    def _L0_gnn_ref(node_features, node_attr, edge_src, edge_dst, edge_attr, edge_scalars, lin1_ws, lin1_wv, fc_w1, fc_w2, sc_ws, sc_wv, lin2_ws, lin2_wv):
        import jax, jax.numpy as jnp
        import numpy as np
        N, E = (1250, 20000)
        S_IN, V_IN = (64, 32)
        S_MID, V_MID = (96, 128)
        S_OUT, V_OUT = (96, 32)
        R = 64
        FC_HID = 64
        W_NUMEL = 64 + 64 + 32 + 32 + 32
        NUM_NEIGHBORS = 16.0

        def _inv(d):
            return 1.0 / jnp.sqrt(jnp.float32(d))

        def _forward(node_features, node_attr, edge_attr, edge_scalars, lin1_ws, lin1_wv, fc_w1, fc_w2, sc_ws, sc_wv, lin2_ws, lin2_wv, edge_src, edge_dst):
            n = node_features.shape[0]
            s = node_features[:, :S_IN]
            v = node_features[:, S_IN:].reshape(n, V_IN, 3)
            a = node_attr
            sc_s = s @ sc_ws * a * _inv(S_IN)
            sc_v = jnp.einsum('nci,cd->ndi', v, sc_wv) * a[:, :, None] * _inv(V_IN)
            h_s = s @ lin1_ws * a * _inv(S_IN)
            h_v = jnp.einsum('nci,cd->ndi', v, lin1_wv) * a[:, :, None] * _inv(V_IN)
            hid = jax.nn.silu(edge_scalars @ fc_w1 * _inv(R))
            w = hid @ fc_w2 * _inv(FC_HID)
            w1, w2, w3, w4, w5 = jnp.split(w, [64, 128, 160, 192], axis=-1)
            es = h_s[edge_src]
            ev = h_v[edge_src]
            e0 = edge_attr[:, :1]
            e1 = edge_attr[:, 1:4]
            m_s1 = w1 * es * e0
            m_s2 = w4 * jnp.einsum('eci,ei->ec', ev, e1) * _inv(3)
            m_v1 = (w2 * es)[:, :, None] * e1[:, None, :]
            m_v2 = w3[:, :, None] * ev * e0[:, :, None]
            m_v3 = w5[:, :, None] * jnp.cross(ev, e1[:, None, :]) * _inv(2)
            mid_s = jnp.concatenate([m_s1, m_s2], axis=-1)
            mid_v = jnp.concatenate([m_v1, m_v2, m_v3], axis=1)
            inv_nn = 1.0 / jnp.sqrt(jnp.float32(NUM_NEIGHBORS))
            agg_s = jax.ops.segment_sum(mid_s, edge_dst, num_segments=n) * inv_nn
            agg_v = jax.ops.segment_sum(mid_v, edge_dst, num_segments=n) * inv_nn
            o_s = agg_s @ lin2_ws * a * _inv(S_MID)
            o_v = jnp.einsum('nci,cd->ndi', agg_v, lin2_wv) * a[:, :, None] * _inv(V_MID)
            pre_s = sc_s + o_s
            pre_v = sc_v + o_v
            scalars = jax.nn.silu(pre_s[:, :64])
            gates = jax.nn.sigmoid(pre_s[:, 64:96])
            gated = gates[:, :, None] * pre_v
            return jnp.concatenate([scalars, gated.reshape(n, 3 * V_OUT)], axis=-1)
        return _forward(node_features, node_attr, edge_attr, edge_scalars, lin1_ws, lin1_wv, fc_w1, fc_w2, sc_ws, sc_wv, lin2_ws, lin2_wv, edge_src, edge_dst)

    def _L1_gnn_ref(node_input, node_attr, node_crystal_attr, sym_mask, edge_attr, edge_length_embedded, edge_src, edge_dst, Ws_sc_a, Wv_sc_a, Ws_sc_c, Wv_sc_c, Ws_l1_a, Wv_l1_a, Ws_l1_c, Wv_l1_c, W_fc1, W_fc2, Ws_l2_a, Wv_l2_a, Ws_l2_c, Wv_l2_c, Ws_l3, Wv_l3):
        import jax, jax.numpy as jnp
        import numpy as np
        N = 25000
        E = 12500
        S = 64
        V = 32
        NB = 10
        H = 100
        WN = 192
        MID = 96
        NUM_NEIGHBORS = 16.0
        C_S = float(np.sin(np.pi / 8.0))
        C_X = float(np.cos(np.pi / 8.0))
        SQRT3 = float(np.sqrt(3.0))

        def fctp_scalar_attr(xs, xv, attr, Ws, Wv):
            s = xs * attr @ Ws
            v = jnp.einsum('nuc,uo->noc', xv * attr[:, :, None], Wv)
            return (s, v)
        n = node_input.shape[0]
        xs = node_input[:, :S]
        xv = node_input[:, S:].reshape(n, V, 3)
        ssa, sva = fctp_scalar_attr(xs, xv, node_attr, Ws_sc_a, Wv_sc_a)
        ssc, svc = fctp_scalar_attr(xs, xv, node_crystal_attr, Ws_sc_c, Wv_sc_c)
        s_s, s_v = (ssa + ssc, sva + svc)
        l1a_s, l1a_v = fctp_scalar_attr(xs, xv, node_attr, Ws_l1_a, Wv_l1_a)
        l1c_s, l1c_v = fctp_scalar_attr(xs, xv, node_crystal_attr, Ws_l1_c, Wv_l1_c)
        x1s, x1v = (l1a_s + l1c_s, l1a_v + l1c_v)
        weight = jax.nn.silu(edge_length_embedded @ W_fc1) @ W_fc2
        w0 = weight[:, :S]
        w1 = weight[:, S:2 * S]
        w2 = weight[:, 2 * S:2 * S + V]
        w3 = weight[:, 2 * S + V:]
        gs = x1s[edge_src]
        gv = x1v[edge_src]
        e_s = edge_attr[:, :1]
        e_v = edge_attr[:, 1:]
        mid0a = w0 * gs * e_s
        mid0b = w3 * (jnp.einsum('euc,ec->eu', gv, e_v) / SQRT3)
        mid1a = w1[:, :, None] * gs[:, :, None] * e_v[:, None, :]
        mid1b = w2[:, :, None] * gv * e_s[:, :, None]
        edge_feat = jnp.concatenate([mid0a, mid0b, mid1a.reshape(-1, 3 * S), mid1b.reshape(-1, 3 * V)], axis=-1)
        agg = jax.ops.segment_sum(edge_feat, edge_dst, num_segments=n) / np.sqrt(NUM_NEIGHBORS)
        m_s = agg[:, :MID]
        m_v = agg[:, MID:].reshape(n, MID, 3)
        l2a_s, l2a_v = fctp_scalar_attr(m_s, m_v, node_attr, Ws_l2_a, Wv_l2_a)
        l2c_s, l2c_v = fctp_scalar_attr(m_s, m_v, node_crystal_attr, Ws_l2_c, Wv_l2_c)
        m_s, m_v = (l2a_s + l2c_s, l2a_v + l2c_v)
        o_s, o_v = fctp_scalar_attr(m_s, m_v, sym_mask, Ws_l3, Wv_l3)
        out_s = C_S * s_s + C_X * o_s
        out_v = C_S * s_v + C_X * o_v
        return jnp.concatenate([out_s, out_v.reshape(n, 3 * V)], axis=-1)
    x = _layernorm(x + _L0_gnn_ref(x, node_vec1, src, dst, edge_attr_4, edge_attr_64, L0_gnn_lin1_ws, L0_gnn_lin1_wv, L0_gnn_fc_w1, L0_gnn_fc_w2, L0_gnn_sc_ws, L0_gnn_sc_wv, L0_gnn_lin2_ws, L0_gnn_lin2_wv), axis=-1)
    x = _layernorm(x + _L1_gnn_ref(x, node_vec1, node_vec1_n2, node_vec1_n3, edge_attr_4, edge_attr_10, src, dst, L1_gnn_Ws_sc_a, L1_gnn_Wv_sc_a, L1_gnn_Ws_sc_c, L1_gnn_Wv_sc_c, L1_gnn_Ws_l1_a, L1_gnn_Wv_l1_a, L1_gnn_Ws_l1_c, L1_gnn_Wv_l1_c, L1_gnn_W_fc1, L1_gnn_W_fc2, L1_gnn_Ws_l2_a, L1_gnn_Wv_l2_a, L1_gnn_Ws_l2_c, L1_gnn_Wv_l2_c, L1_gnn_Ws_l3, L1_gnn_Wv_l3), axis=-1)
    return x

_drawn_inputs = setup_inputs


def setup_inputs(seed=0):
    import zlib

    import numpy as np

    out = dict(_drawn_inputs(seed))
    spreads = {}
    factors = {}
    for name, (base, spread) in spreads.items():
        noise = np.random.default_rng([zlib.crc32(name.encode()), seed]).standard_normal(out[name].shape)
        drawn = base * np.exp(spread * noise) if base else spread * noise
        out[name] = jnp.asarray(drawn.astype(out[name].dtype))
    for name, factor in factors.items():
        out[name] = (out[name] * factor).astype(out[name].dtype)
    return out
```

```python
import math
from contextlib import ExitStack

import concourse.bass as bass
from concourse import mybir
from concourse.alu_op_type import AluOpType as ALU

F32 = mybir.dt.float32
I32 = mybir.dt.int32
ACT = mybir.ActivationFunctionType
AX = mybir.AxisListType

P = 128
TILE = 128
GROUP = 2 * TILE
Q = 4
ITER = Q * GROUP
WIN = 16
NB = 5
S, V = 64, 32
D = S + 3 * V
EPS = 1e-5
INV_SQRT = lambda d: 1.0 / float(d) ** 0.5


class Layer:

    def __init__(self, name, vector_products, hidden):
        self.name = name
        self.k = vector_products
        self.wn = 2 * S + V * self.k
        self.hidden = hidden
        self.pn = 2 * S + 3 * V * self.k
        self.chunks = [(0, (0, 4), 0), (P, (0, 1), 1 + 3 * self.k)]
        self.chunks += [(min(P + 3 * V * m, self.pn - P), (1, 4), 1 + 3 * m) for m in range(1, self.k)]
        self.units = 2 + 3 * self.k
        self.u_last = 1 + 3 * self.k

    def row(self, chunk, product):
        return product - self.chunks[chunk][0]


def gnn_kernel(nc, ins, out, n_nodes, n_edges):
    n_iter = -(-n_edges // ITER)
    n_groups = n_iter * Q
    n_tiles = 2 * n_groups
    n_steps = -(-n_nodes // (NB * P))
    n_pad = n_steps * NB * P
    n_win = -(-n_nodes // WIN)
    assert n_iter >= 3 and n_nodes + WIN - 1 <= n_pad

    L0 = Layer("l0", 3, 64)
    L1 = Layer("l1", 2, 100)
    U0, U1 = L0.units, L1.units

    R0S, R0V = 0, 4 * 96
    R0_COLS = 4 * 96 + 4 * 96 + 3 * 32
    R1S, R1V = 0, 4 * 128
    R1_COLS = 4 * 128 + 192 + 3 * 64

    with ExitStack() as ctx:
        def sb(name, shape, dt=F32):
            return ctx.enter_context(nc.sbuf_tensor(name, shape, dt))

        def sem(name):
            return ctx.enter_context(nc.semaphore(name))

        acc = sb("acc", [P, n_pad * U0])
        src = sb("src", [P, n_tiles], I32)
        attr = sb("attr", [P, n_tiles, 4])
        rel = sb("rel", [P, n_groups, 2])
        first = sb("first", [P, n_groups], I32)
        flag = sb("flag", [P, 8], I32)
        iota = sb("iota", [P, WIN])
        window = sb("window", [P, WIN])
        ident = sb("ident", [P, P])
        w1_0 = sb("w1_0", [P, P])
        w2_0 = sb("w2_0", [P, 2, L0.wn])
        w1_1 = sb("w1_1", [P, 100])
        w2_1 = sb("w2_1", [P, L1.wn])
        lin0 = sb("lin0", [P, 2 * 96])
        self0 = sb("self0", [P, 2 * 96])
        lin1s = sb("lin1s", [P, 4 * S])
        lin1v = sb("lin1v", [P, 4 * 96])
        r0 = sb("r0", [P, R0_COLS])
        r1 = sb("r1", [P, R1_COLS])
        edge_in = sb("edge_in", [P, ITER])
        hidden = sb("hidden", [P, ITER])
        idx = sb("idx", [P, 2 * Q], I32)
        work = sb("work", [P, 5760])
        prod = work[:, 0:Q * 2 * L0.pn].rearrange("p (q h c) -> p q h c", q=Q, h=2)
        o = Q * 2 * L0.pn
        rows = work[:, o:o + Q * 2 * D].rearrange("p (q h c) -> p q h c", q=Q, h=2)
        o += Q * 2 * D
        hot = work[:, o:o + Q * 2 * WIN].rearrange("p (q h n) -> p q h n", q=Q, h=2)
        o += Q * 2 * WIN
        whot = work[:, o:o + Q * 8 * WIN].rearrange("p (q h n k) -> p q h n k", q=Q, h=2, k=4)
        assert o + Q * 8 * WIN <= 5760
        stage = work[:, 0:U0 * P]
        o = U0 * P
        xs_flat, xv_flat = work[0:S, o:o + NB * P], work[0:96, o + NB * P:o + 2 * NB * P]
        xs, xv = (a.rearrange("p (t n) -> p t n", t=NB) for a in (xs_flat, xv_flat))
        o += 2 * NB * P
        x_rows = work[:, o:o + NB * D].rearrange("p (t c) -> p t c", t=NB)
        o += NB * D
        z = work[:, o:o + NB * D].rearrange("p (t c) -> p t c", t=NB)
        o += NB * D
        pre = work[:, o:o + NB * 192].rearrange("p (t c) -> p t c", t=NB)
        h_out = work[:, o:o + NB * D].rearrange("p (t c) -> p t c", t=NB)
        o += NB * 192
        assert o <= 5760
        gates = sb("gates", [P, NB, 96])
        coef = sb("coef", [P, 4, NB])
        am = sb("am", [P, 2, NB])
        stat = sb("stat", [P, 4, NB])
        eps = sb("eps", [P, 1])


        ps = ctx.enter_context(nc.psum_tensor("ps", [P, 8 * 512], F32))
        bank = [ps[:, 512 * b:512 * b + 512] for b in range(8)]
        hid_ps = ps[:, 0:2 * 512]
        half = [ps[:, 512 * b:512 * b + NB * 256].rearrange("p (t c) -> p t c", t=NB) for b in (0, 3)]

        h_dram = [nc.dram_tensor(f"h{l}_rows", [n_pad, D], F32).ap() for l in range(2)]
        base_dram = nc.dram_tensor("base_rows", [n_pad, D], F32).ap()

        loaded = sem("loaded")
        cleared = sem("cleared")
        weights_landed = sem("weights_landed")
        weights_scaled = sem("weights_scaled")
        first_cast = sem("first_cast")
        first_spread = sem("first_spread")
        setup_step = sem("setup_step")
        far_found = sem("far_found")
        far_turned = sem("far_turned")
        flag_ready = sem("flag_ready")
        flag_spread = sem("flag_spread")
        comp_ready = sem("comp_ready")
        comp_scaled = sem("comp_scaled")
        comp_placed = sem("comp_placed")
        acc_zeroed = sem("acc_zeroed")
        edges_done = [sem(f"edges_done{l}") for l in range(2)]
        n0_in, n0_mm, n0_out, n0_stored = sem("n0_in"), sem("n0_mm"), sem("n0_out"), sem("n0_stored")
        n1_in, n1_staged, n1_tile = sem("n1_in"), sem("n1_staged"), sem("n1_tile")
        n1_scaled, n1_gates, n1_x1 = sem("n1_scaled"), sem("n1_gates"), sem("n1_x1")
        n1_turned, n1_copied = sem("n1_turned"), sem("n1_copied")
        n1_h_mm, n1_h_used, n1_self_mm, n1_self_used = (sem("n1_h_mm"), sem("n1_h_used"), sem("n1_self_mm"),
                                                        sem("n1_self_used"))
        n1_stored = sem("n1_stored")
        n2_in, n2_staged, n2_tile, n2_scaled = sem("n2_in"), sem("n2_staged"), sem("n2_tile"), sem("n2_scaled")
        n2_out, n2_stored = sem("n2_out"), sem("n2_stored")
        chain = [sem("n1_chain"), sem("n2_chain")]
        var_ready = [sem("n1_var"), sem("n2_var")]
        std_ready = [sem("n1_std"), sem("n2_std")]

        passed = sem("passed")

        block = ctx.enter_context(nc.Block())

        def wait(eng, s, value):
            if not isinstance(value, int) or value > 0:
                eng.wait_ge(s, value)

        def hold(eng, s, value):
            if not isinstance(value, int) or value > 0:
                eng.wait_ge(s, value)
                eng.sem_inc(passed, 1)

        def looped(eng, count, body, peel_last=False):
            body(0)
            end = count - 1 if peel_last else count
            if end > 1:
                with eng.Fori(1, end) as i:
                    body(i)
            if peel_last:
                body(count - 1)

        def spread(ap, axis, n):
            ap = ap.unsqueeze(axis)
            shape = list(ap.shape)
            shape[axis] = n
            return ap.to_broadcast(shape)

        placed = [
            (w1_0[0:64, 0:64], ins["L0_gnn_fc_w1"]), (w1_0[64:128, 64:128], ins["L0_gnn_fc_w1"]),
            (w2_0[0:64, 0], ins["L0_gnn_fc_w2"]), (w2_0[64:128, 1], ins["L0_gnn_fc_w2"]),
            (w1_1[0:10, :], ins["L1_gnn_W_fc1"]), (w2_1[0:100, :], ins["L1_gnn_W_fc2"]),
            (lin0[0:S, 0:S], ins["L0_gnn_lin1_ws"]), (self0[0:S, 0:96], ins["L0_gnn_sc_ws"]),
            (r0[0:S, R0S:R0S + 96], ins["L0_gnn_lin2_ws"][0:64]),
        ]
        for i in range(3):
            placed += [
                (lin0[V * i:V * i + V, 96 + V * i:96 + V * i + V], ins["L0_gnn_lin1_wv"]),
                (self0[V * i:V * i + V, 96 + V * i:96 + V * i + V], ins["L0_gnn_sc_wv"]),
            ]
        for m, part in enumerate(("l1_a", "l1_c", "sc_a", "sc_c")):
            placed.append((lin1s[0:S, m * S:m * S + S], ins[f"L1_gnn_Ws_{part}"]))
            for i in range(3):
                placed.append((lin1v[V * i:V * i + V, m * 96 + V * i:m * 96 + V * i + V], ins[f"L1_gnn_Wv_{part}"]))
        signs = []
        c_chunk, d_chunk = 2, 3
        for k in range(3):
            r = L0.row(c_chunk, P + 3 * V + V * k)
            col = R0S + 96 * (1 + k)
            placed.append((r0[r:r + V, col:col + 96], ins["L0_gnn_lin2_ws"][64:96]))
            placed.append((r0[V * k:V * k + V, R0V + V * k:R0V + V * k + V], ins["L0_gnn_lin2_wv"][64:96]))
            for j, i, sign in (((k + 1) % 3, (k + 2) % 3, 1), ((k + 2) % 3, (k + 1) % 3, -1)):
                r = L0.row(d_chunk, P + 6 * V + V * i)
                col = R0V + 96 * (1 + k) + V * j
                placed.append((r0[r:r + V, col:col + V], ins["L0_gnn_lin2_wv"][96:128]))
                signs.append((col, sign))
            col = R0V + 4 * 96 + V * k
            placed.append((r0[64:128, col:col + V], ins["L0_gnn_lin2_wv"][0:64]))
        l2t, l3, comp = work[0:96, 0:4 * 96], work[0:96, 384:384 + 96], work[0:96, 512:512 + 192]
        for m, part in enumerate(("Ws_l2_a_t", "Ws_l2_c_t", "Wv_l2_a_t", "Wv_l2_c_t")):
            placed.append((l2t[:, 96 * m:96 * m + 96], ins[part]))
        placed += [(l3[:, 0:S], ins["L1_gnn_Ws_l3"]), (l3[:, S:96], ins["L1_gnn_Wv_l3"])]
        comp_parts = [(r1[0:64, R1S:R1S + 128], comp[0:64, 0:128])]
        for k in range(3):
            r = L1.row(2, P + 3 * V + V * k)
            col = R1S + 128 * (1 + k)
            comp_parts.append((r1[r:r + V, col:col + 128], comp[64:96, 0:128]))
            for m in range(2):
                col = R1V + 96 * m + V * k
                comp_parts.append((r1[V * k:V * k + V, col:col + V], comp[64:96, 128 + V * m:128 + V * m + V]))
            col = R1V + 192 + 64 * k
            comp_parts.append((r1[64:128, col:col + 64], comp[0:64, 128:192]))

        dst_i = acc[:, 0:n_tiles].bitcast(I32)
        dst_f = acc[:, n_tiles:2 * n_tiles]
        far = acc[:, 2 * n_tiles:3 * n_tiles]
        first_f = acc[0:1, 3 * n_tiles:3 * n_tiles + n_groups]
        o = 3 * n_tiles + n_groups
        far_max = acc[:, o:o + 1]
        far_row = acc[0:1, o + 1:o + 2]
        flag_f = acc[0:1, o + 2:o + 3]
        flag_all = acc[:, o + 3:o + 4]
        ones = acc[0:1, o + 4:o + 4 + P]
        SCRATCH = o + 4 + P
        assert n_groups <= 512 and SCRATCH <= n_pad * U1
        first_bc = bank[7][:, 0:n_groups]

        tables = [(dst_i, ins["dst"]), (first[0:1, :], ins["first"]), (iota[:], ins["iota"]),
                  (ident[:], ins["ident"]), (src[:], ins["src"]), (attr[:], ins["attr"])]
        clears = [w1_0[:], w2_0[:], lin0[:], self0[:], lin1v[:], r0[:], r1[:]]

        c0 = INV_SQRT(64) * INV_SQRT(16)
        c1 = INV_SQRT(16)
        C_S, C_X = math.sin(math.pi / 8.0), math.cos(math.pi / 8.0)
        scaled = [
            (lin0[0:S, 0:S], INV_SQRT(S)), (lin0[0:96, 96:192], INV_SQRT(V)),
            (self0[0:S, 0:96], INV_SQRT(S)), (self0[0:96, 96:192], INV_SQRT(V)),
            (r0[:, R0S:R0S + 96], c0 * INV_SQRT(96)),
            (r0[:, R0S + 96:R0S + 384], c0 * INV_SQRT(96) * INV_SQRT(3)),
            (r0[:, R0V:R0V + 96], c0 * INV_SQRT(128)),
            (r0[:, R0V + 384:R0V + 480], c0 * INV_SQRT(128)),
            (lin1s[0:S, 2 * S:4 * S], C_S), (lin1v[0:96, 192:384], C_S),
        ] + [(r0[:, col:col + V], sign * c0 * INV_SQRT(128) * INV_SQRT(2)) for col, sign in signs]


        def at(ap, j):
            if isinstance(j, int):
                return ap[j]
            ap = ap[bass.ds(j, 1)]
            return ap.rearrange("o p c -> (o p) c" if len(ap.shape) == 3 else "o p t c -> (o p) t c")

        def step_rows(dram):
            return dram.rearrange("(j t p) c -> j p t c", t=NB, p=P)

        def coef_of(m):
            return coef[:, m]

        def stage_tiles(act, layer, staged, used, j):
            U = layer.units
            for t in range(NB):
                c = j * NB + t
                wait(act, used, c)
                s = acc[:, c * (U * P):(c + 1) * (U * P)] if isinstance(c, int) else \
                    acc[:, bass.ds(c * (U * P), U * P)]
                act.activation(stage[:, 0:U * P], s, ACT.Copy).then_inc(staged, 1)

        def unit(layer, u):
            return stage[:, 0:layer.units * P].rearrange("p (n u) -> p n u", u=layer.units)[:, :, u]

        def norm(dve, l, j, link):
            link(dve.tensor_reduce(stat[:, 0], z, AX.X, ALU.add))
            link(dve.tensor_scalar(stat[:, 1], stat[:, 0], 1.0 / D, None, ALU.mult))
            link(dve.tensor_tensor(z, z, spread(stat[:, 1], 2, D), ALU.subtract))
            link(dve.tensor_tensor(h_out, z, z, ALU.mult))
            dve.tensor_reduce(stat[:, 2], h_out, AX.X, ALU.add).then_inc(var_ready[l], 1)
            dve.wait_ge(std_ready[l], j + 1)
            link(dve.reciprocal(stat[:, 0], stat[:, 3]))

        def deviation(act, l, j):
            act.wait_ge(var_ready[l], j + 1)
            act.activation(stat[:, 3], stat[:, 2], ACT.Sqrt, bias=eps[:], scale=1.0 / D).then_inc(std_ready[l], 1)

        class Link:

            def __init__(self, eng, s, start):
                self.eng, self.s, self.start, self.n = eng, s, start, 0

            def __call__(self, ins_):
                self.n += 1
                ins_.then_inc(self.s, 1)
                self.eng.wait_ge(self.s, self.start + self.n)

        class Edge:
            def __init__(self, n):
                self.loaded = sem(f"e{n}_loaded")
                self.mixed = sem(f"e{n}_mixed")
                self.hidden = sem(f"e{n}_hidden")
                self.weights = sem(f"e{n}_weights")
                self.index = sem(f"e{n}_index")
                self.rows = [sem(f"e{n}_rows{q}") for q in range(Q)]
                self.hot = sem(f"e{n}_hot")
                self.whot = sem(f"e{n}_whot")
                self.prod = sem(f"e{n}_prod")
                self.agg = sem(f"e{n}_agg")
                self.added = sem(f"e{n}_added")
                self.window = sem(f"e{n}_window")

        edge = [Edge(0), Edge(1)]
        edge_feats = [ins["edge64"], ins["edge10"]]

        def edge_loads(sp, l):
            e = edge[l]
            used = P if l == 0 else 10
            cols = ITER // 2 if l == 0 else ITER

            def load(i):
                s = edge_feats[l][i] if isinstance(i, int) else \
                    edge_feats[l][bass.ds(i, 1)].rearrange("o p c -> (o p) c")
                sp.dma_start(edge_in[0:used, 0:cols], s).then_inc(e.loaded, 16)

            load(0)
            with sp.Fori(1, n_iter) as i:
                hold(sp, e.mixed, i)
                load(i)

        def edge_gathers(pool, l):
            e = edge[l]

            def body(i):
                for q in range(Q):
                    n = i * Q + q
                    wait(pool, e.prod, n - Q + 1)
                    col = 2 * n
                    s = src[:, col:col + 2] if isinstance(i, int) else src[:, bass.ds(col, 2)]
                    pool.tensor_copy(idx[:, 2 * q:2 * q + 2], s).then_inc(e.index, 1)
                    pool.wait_ge(e.index, 1)
                    pool.sem_inc(e.index, -1)
                    for h in range(2):
                        pool.indirect_dma_start(
                            out=rows[:, q, h], out_offset=None, in_=h_dram[l],
                            in_offset=bass.IndirectOffsetOnAxis(ap=idx[:, 2 * q + h:2 * q + h + 1], axis=0),
                        ).then_inc(e.rows[q], 16)

            looped(pool, n_iter, body)

        def edge_silu(act, l):
            e = edge[l]
            parts = P if l == 0 else 100
            wide = P if l == 0 else GROUP
            scale = INV_SQRT(64) if l == 0 else 1.0

            def body(i):
                for q in range(Q):
                    if q == 0:
                        act.wait_ge(e.mixed, i + 1)
                    wait(act, e.weights, (i - 1) * Q + q + 1)
                    s = hid_ps[0:parts, q * wide:(q + 1) * wide]
                    act.activation(hidden[0:parts, q * wide:(q + 1) * wide], s, ACT.Silu,
                                   scale=scale).then_inc(e.hidden, 1)

            looped(act, n_iter, body)

        def edge_tensor(pe, l, layer, general):
            e = edge[l]
            lag = 0 if general else 2

            def mix(i):
                pe.wait_ge(e.loaded, 16 * i + 16)
                wait(pe, e.hidden, Q * i)
                if l == 0:
                    pe.matmul(bank[0], w1_0[:], edge_in[:, 0:512], start=True, stop=True).then_inc(e.mixed, 1)
                else:
                    pe.matmul(bank[0][0:100], w1_1[0:10], edge_in[0:10, 0:512], start=True, stop=True)
                    pe.matmul(bank[1][0:100], w1_1[0:10], edge_in[0:10, 512:1024], start=True,
                              stop=True).then_inc(e.mixed, 1)

            def radial(i, q):
                pe.wait_ge(e.hidden, i * Q + q + 1)
                wait(pe, e.prod, i * Q + q - 1)
                if l == 0:
                    pe.matmul(bank[2 + q % 2][:, 0:2 * layer.wn], hidden[:, q * P:(q + 1) * P],
                              w2_0[:].rearrange("p h c -> p (h c)"), start=True, stop=True).then_inc(e.weights, 1)
                else:
                    for h in range(2):
                        c = (2 * q + h) * P
                        mm = pe.matmul(bank[2 + q % 2][:, h * layer.wn:(h + 1) * layer.wn],
                                       hidden[0:100, c:c + P], w2_1[0:100], start=True, stop=True)
                    mm.then_inc(e.weights, 1)

            def sums(n, q, slot):
                pe.wait_ge(e.whot, n + 1)
                wait(pe, e.added, n - 1)
                o = bank[4 + slot][:, 0:WIN * layer.units].rearrange("p (n u) -> p n u", u=layer.units)
                for c, (a, b), u in layer.chunks:
                    for h in range(2):
                        mm = pe.matmul(o[:, :, u:u + b - a],
                                       prod[:, q, h, c:c + P], whot[:, q, h, :, a:b],
                                       start=(h == 0), stop=(h == 1))
                mm.then_inc(e.agg, 1)

            def body(i, last=False):
                for q in range(Q):
                    radial(i, q)
                    if q == 1 and not last:
                        mix(i + 1)
                    n = i * Q + q - lag
                    if general:
                        hold(pe, e.prod, n + 1)
                        with pe.Fori(0, n_win) as w:
                            pe.wait_ge(e.whot, n * n_win + w + 1)
                            o = bank[4][:, 0:WIN * layer.units].rearrange("p (n u) -> p n u", u=layer.units)
                            for c, (a, b), u in layer.chunks:
                                for h in range(2):
                                    mm = pe.matmul(o[:, :, u:u + b - a],
                                                   prod[:, q, h, c:c + P], whot[:, q, h, :, a:b],
                                                   start=(h == 0), stop=(h == 1))
                            mm.then_inc(e.agg, 1)
                    elif not isinstance(n, int) or n >= 0:
                        pe.wait_ge(e.prod, n + 1)
                        sums(n, (q - lag) % Q, (q - lag) % 2)

            mix(0)
            body(0)
            with pe.Fori(1, n_iter - 1) as i:
                body(i)
            body(n_iter - 1, last=True)
            for n in range(n_groups - lag, n_groups):
                pe.wait_ge(e.prod, n + 1)
                sums(n, n % Q, n % 2)

        def edge_vector(dve, l, layer, general):
            e = edge[l]
            U = layer.units
            lag = 3

            def tile_cols(ap, n, size):
                if isinstance(n, int):
                    return ap[:, n * size:(n + 1) * size]
                return ap[:, bass.ds(n * size, size)]

            def weighted_hot(n, q, count, nodes):
                r = rel[:, n] if isinstance(n, int) else rel[:, bass.ds(n, 1)].rearrange("p o h -> p (o h)")
                dve.tensor_tensor(hot[:, q], spread(nodes, 1, 2), spread(r, 2, WIN), ALU.is_equal).then_inc(e.hot, 1)
                dve.wait_ge(e.hot, count + 1)
                a = tile_cols(attr[:].rearrange("p t k -> p (t k)"), n, 8).rearrange("p (h k) -> p h k", k=4)
                dve.tensor_tensor(whot[:, q], spread(hot[:, q], 3, 4), spread(a, 2, WIN),
                                  ALU.mult).then_inc(e.whot, 1)

            def products(i, q, n):
                dve.wait_ge(e.rows[q], 32 * i + 32)
                dve.wait_ge(e.weights, n + 1)
                w = bank[2 + q % 2][:, 0:2 * layer.wn].rearrange("p (h c) -> p h c", h=2)
                dve.tensor_tensor(prod[:, q, :, 0:2 * S].rearrange("p h (k c) -> p h k c", k=2),
                                  w[:, :, 0:2 * S].rearrange("p h (k c) -> p h k c", k=2),
                                  spread(rows[:, q, :, 0:S], 2, 2), ALU.mult)
                for h in range(2):
                    ins_ = dve.tensor_tensor(
                        prod[:, q, h, 2 * S:layer.pn].rearrange("p (k i c) -> p k i c", k=layer.k, i=3),
                        spread(w[:, h, 2 * S:layer.wn].rearrange("p (k c) -> p k c", k=layer.k), 2, 3),
                        spread(rows[:, q, h, S:D].rearrange("p (i c) -> p i c", i=3), 1, layer.k), ALU.mult)
                ins_.then_inc(e.prod, 1)

            def add(count, slot, offset):
                dve.wait_ge(e.agg, count + 1)
                wait(dve, e.added, count)
                a = acc[:, bass.ds(offset, WIN * U)]
                dve.tensor_tensor(a, a, bank[4 + slot][:, 0:WIN * U], ALU.add).then_inc(e.added, 1)

            def window_start(n):
                s = first[0:1, n:n + 1] if isinstance(n, int) else first[0:1, bass.ds(n, 1)]
                return dve.value_load(s, min_val=0, max_val=n_nodes - 1) * U

            def body(i):
                for q in range(Q):
                    n = i * Q + q
                    if not general:
                        wait(dve, e.agg, n - Q + 1)
                        weighted_hot(n, q, n, iota[:])
                        products(i, q, n)
                        m = n - lag
                        if not isinstance(m, int) or m >= 0:
                            add(m, (q - lag) % 2, window_start(m))
                        continue
                    products(i, q, n)
                    dve.tensor_copy(window[:], iota[:]).then_inc(e.window, 1)
                    hold(dve, e.window, n * (n_win + 1) + 1)
                    with dve.Fori(0, n_win) as w:
                        count = n * n_win + w
                        weighted_hot(n, q, count, window[:])
                        dve.wait_ge(e.agg, count + 1)
                        a = acc[:, bass.ds(w * (WIN * U), WIN * U)]
                        dve.tensor_tensor(a, a, bank[4][:, 0:WIN * U], ALU.add).then_inc(e.added, 1)
                        dve.wait_ge(e.added, count + 1)
                        dve.tensor_scalar(window[:], window[:], float(WIN), None, ALU.add).then_inc(e.window, 1)
                        dve.wait_ge(e.window, n * (n_win + 1) + w + 2)

            looped(dve, n_iter, body)
            if not general:
                for m in range(n_groups - lag, n_groups):
                    add(m, m % 2, window_start(m))
                dve.wait_ge(e.added, n_groups)
            dve.sem_inc(edges_done[l], 1)

        LOADS0, LOADS1, LOADS2 = 3 * 16, 4 * 16, 2 * 16
        LINKS1, LINKS2 = 8 + 2 * NB, 8

        @block.sync
        def _(sp):
            for tile, s in tables:
                sp.dma_start(tile, s).then_inc(loaded, 16)
            sp.wait_ge(cleared, len(clears))
            for tile, s in placed:
                sp.dma_start(tile, s).then_inc(weights_landed, 16)

            def rows0(j):
                hold(sp, n0_out, j)
                sp.dma_start(xs_flat, at(ins["xs"], j)).then_inc(n0_in, 16)
                sp.dma_start(xv_flat, at(ins["xv"], j)).then_inc(n0_in, 16)
                sp.dma_start(coef[:, 0:3], at(ins["coef"], j)).then_inc(n0_in, 16)
                hold(sp, n0_out, j + 1)
                sp.dma_start(at(step_rows(h_dram[0]), j), h_out).then_inc(n0_stored, 16)

            looped(sp, n_steps, rows0)
            sp.wait_ge(comp_scaled, 3)
            for tile, s in comp_parts:
                sp.dma_start(tile, s).then_inc(comp_placed, 16)
            edge_loads(sp, 0)

            sp.wait_ge(edges_done[0], 1)
            sp.wait_ge(comp_placed, 16 * len(comp_parts))

            def rows1(j):
                sp.dma_start(xs_flat, at(ins["xs"], j)).then_inc(n1_in, 16)
                sp.dma_start(xv_flat, at(ins["xv"], j)).then_inc(n1_in, 16)
                sp.dma_start(coef[:, 0:3], at(ins["coef"], j)).then_inc(n1_in, 16)
                sp.dma_start(x_rows, at(step_rows(ins["x_rows"]), j)).then_inc(n1_in, 16)
                hold(sp, n1_h_used, NB * j + NB)
                hold(sp, n1_self_used, NB * j + NB)
                sp.dma_start(at(step_rows(h_dram[1]), j), h_out).then_inc(n1_stored, 16)
                sp.dma_start(at(step_rows(base_dram), j), x_rows).then_inc(n1_stored, 16)
                hold(sp, n1_stored, 32 * j + 32)

            looped(sp, n_steps, rows1)
            edge_loads(sp, 1)

            sp.wait_ge(edges_done[1], 1)

            def rows2(j):
                sp.dma_start(coef[:, 0:3], at(ins["coef"], j)).then_inc(n2_in, 16)
                sp.dma_start(x_rows, at(step_rows(base_dram), j)).then_inc(n2_in, 16)
                hold(sp, n2_out, 2 * j + 2)
                sp.dma_start(at(step_rows(out), j), h_out).then_inc(n2_stored, 16)

            looped(sp, n_steps, rows2)
            sp.wait_ge(n2_stored, 16 * n_steps)

        @block.gpsimd
        def _(pool):
            pool.memset(acc[:, SCRATCH:], 0.0).then_inc(acc_zeroed, 1)
            pool.wait_ge(n0_stored, 16 * n_steps)
            pool.wait_ge(comp_placed, 16 * len(comp_parts))
            pool.wait_ge(loaded, 16 * len(tables))
            edge_gathers(pool, 0)
            cols = n_pad * U1
            a = 0
            for t in range(n_steps):
                b = min((t + 1) * NB * P * U0, cols)
                pool.wait_ge(n1_staged, NB * (t + 1))
                if a < b:
                    pool.memset(acc[:, a:b], 0.0).then_inc(acc_zeroed, 1)
                a = max(a, b)
            pool.wait_ge(n1_stored, 32 * n_steps)
            edge_gathers(pool, 1)

        zero_parts = len([t for t in range(n_steps) if t * NB * P * U0 < n_pad * U1])

        @block.scalar
        def _(act):
            edge_silu(act, 0)
            act.wait_ge(edges_done[0], 1)

            def step1(j):
                stage_tiles(act, L0, n1_staged, n1_tile, j)
                act.wait_ge(n1_scaled, j + 1)
                act.activation(gates[:], pre[:, :, 0:96], ACT.Sigmoid).then_inc(n1_gates, 1)
                deviation(act, 0, j)
                act.wait_ge(n1_turned, j + 1)
                act.activation(xs, half[1][0:S, :, 0:P], ACT.Copy).then_inc(n1_copied, 1)
                act.activation(xv, half[1][0:96, :, P:2 * P], ACT.Copy).then_inc(n1_copied, 1)

            looped(act, n_steps, step1)
            edge_silu(act, 1)
            act.wait_ge(edges_done[1], 1)

            def step2(j):
                stage_tiles(act, L1, n2_staged, n2_tile, j)
                deviation(act, 1, j)

            looped(act, n_steps, step2)

        def branched(eng, edges, l, layer):
            eng.wait_ge(flag_ready, 1)
            far_flag = eng.value_load(flag[0:1, 0:1], min_val=0, max_val=1)
            with eng.If(far_flag < 1):
                edges(eng, l, layer, False)
            with eng.Else():
                edges(eng, l, layer, True)

        @block.tensor
        def _(pe):
            pe.wait_ge(first_cast, 2)
            pe.matmul(first_bc, ones, first_f, start=True, stop=True).then_inc(first_spread, 1)
            pe.wait_ge(far_found, 1)
            pe.wait_ge(loaded, 16 * len(tables))
            pe.matmul(bank[6][0:1, 0:P], far_max, ident[:], start=True, stop=True).then_inc(far_turned, 1)
            pe.wait_ge(flag_ready, 1)
            pe.matmul(bank[5][:, 0:1], ones, flag_f, start=True, stop=True).then_inc(flag_spread, 1)
            pe.wait_ge(weights_landed, 16 * len(placed))
            for m in range(4):
                a, b = ((0, S), (0, S), (S, 96), (S, 96))[m]
                c = (0, 64, 128, 160)[m]
                mm = pe.matmul(bank[4][0:96, c:c + b - a], l2t[:, 96 * m:96 * m + 96], l3[:, a:b], start=True,
                               stop=True)
            mm.then_inc(comp_ready, 1)
            pe.wait_ge(weights_scaled, len(scaled))

            def rows0(j):
                pe.wait_ge(n0_in, LOADS0 * j + LOADS0)
                wait(pe, n0_out, j)
                for t in range(NB):
                    pe.matmul(half[0][:, t, 0:S], xs[:, t], lin0[0:S, 0:S], start=True, stop=True)
                    mm = pe.matmul(half[0][:, t, S:D], xv[:, t], lin0[0:96, 96:192], start=True, stop=True)
                mm.then_inc(n0_mm, 1)

            looped(pe, n_steps, rows0)
            pe.wait_ge(n0_out, n_steps)
            branched(pe, edge_tensor, 0, L0)
            pe.wait_ge(edges_done[0], 1)

            def rows1(j):
                pe.wait_ge(n1_in, LOADS1 * j + LOADS1)
                wait(pe, n1_scaled, j)
                for t in range(NB):
                    c = j * NB + t
                    o = half[0][:, t]
                    pe.wait_ge(n1_staged, c + 1)
                    pe.matmul(o[:, 0:96], xs[:, t], self0[0:S, 0:96], start=True, stop=False)
                    for m, u in enumerate((0, 4, 5, 6)):
                        pe.matmul(o[:, 0:96], unit(L0, u), r0[:, R0S + 96 * m:R0S + 96 * m + 96], start=False,
                                  stop=(m == 3))
                    pe.matmul(o[:, 96:192], xv[:, t], self0[0:96, 96:192], start=True, stop=False)
                    for m, u in enumerate((10, 7, 8, 9)):
                        pe.matmul(o[:, 96:192], unit(L0, u), r0[:, R0V + 96 * m:R0V + 96 * m + 96], start=False,
                                  stop=False)
                    for k in range(3):
                        mm = pe.matmul(o[:, 96 + V * k:96 + V * k + V], unit(L0, 1 + k),
                                       r0[:, R0V + 384 + V * k:R0V + 384 + V * k + V], start=False, stop=(k == 2))
                    mm.then_inc(n1_tile, 1)
                pe.wait_ge(n1_x1, j + 1)
                for t in range(NB):
                    pe.transpose(half[1][0:96, t, P:2 * P], z[:, t, S:D], ident[:])
                    mm = pe.transpose(half[1][0:S, t, 0:P], z[:, t, 0:S], ident[:])
                mm.then_inc(n1_turned, 1)
                pe.wait_ge(n1_copied, 2 * j + 2)
                for t in range(NB):
                    c = j * NB + t
                    for m, used, done in ((0, n1_h_used, n1_h_mm), (1, n1_self_used, n1_self_mm)):
                        o = bank[6 + m][:, 0:2 * D].rearrange("p (m c) -> p m c", m=2)
                        wait(pe, used, c)
                        pe.matmul(o[:, :, 0:S], xs[:, t], lin1s[0:S, 2 * S * m:2 * S * m + 2 * S], start=True,
                                  stop=True)
                        pe.matmul(o[:, :, S:D], xv[:, t], lin1v[0:96, 192 * m:192 * m + 192], start=True,
                                  stop=True).then_inc(done, 1)

            looped(pe, n_steps, rows1)
            branched(pe, edge_tensor, 1, L1)
            pe.wait_ge(edges_done[1], 1)

            def rows2(j):
                wait(pe, n2_scaled, 2 * j)
                for t in range(NB):
                    pe.wait_ge(n2_staged, j * NB + t + 1)
                    o = bank[t][:, 0:2 * D].rearrange("p (m c) -> p m c", m=2)
                    for m, u in enumerate((0, 4, 5, 6)):
                        pe.matmul(o[:, :, 0:S], unit(L1, u), r1[:, R1S + 128 * m:R1S + 128 * m + 128],
                                  start=(m == 0), stop=(m == 3))
                    pe.matmul(o[:, :, S:D], unit(L1, 7), r1[:, R1V:R1V + 192], start=True, stop=False)
                    for k in range(3):
                        c = R1V + 192 + 64 * k
                        mm = pe.matmul(o[:, :, S + V * k:S + V * k + V], unit(L1, 1 + k), r1[:, c:c + 64],
                                       start=False, stop=(k == 2))
                    mm.then_inc(n2_tile, 1)

            looped(pe, n_steps, rows2)

        @block.vector
        def _(dve):
            for tile in clears:
                dve.memset(tile, 0.0).then_inc(cleared, 1)
            dve.memset(eps[:], EPS).then_inc(setup_step, 1)
            dve.memset(ones, 1.0).then_inc(first_cast, 1)
            dve.wait_ge(loaded, 16 * len(tables))
            link = Link(dve, setup_step, 1)
            dve.tensor_copy(first_f, first[0:1, :]).then_inc(first_cast, 1)
            link(dve.tensor_copy(dst_f, dst_i))
            dve.wait_ge(first_spread, 1)
            rel_groups = rel[:]
            link(dve.tensor_tensor(rel_groups, dst_f.rearrange("p (g h) -> p g h", h=2), spread(first_bc, 2, 2),
                                   ALU.subtract))
            middle = (WIN - 1) / 2
            link(dve.tensor_scalar(far, rel_groups.rearrange("p g h -> p (g h)"), middle, None, ALU.subtract))
            link(dve.tensor_tensor(far, far, far, ALU.mult))
            dve.tensor_reduce(far_max, far, AX.X, ALU.max).then_inc(far_found, 1)
            dve.wait_ge(far_turned, 1)
            link(dve.tensor_reduce(far_row, bank[6][0:1, 0:P], AX.X, ALU.max))
            link(dve.tensor_scalar(flag_f, far_row, (middle + 0.5) ** 2, None, ALU.is_gt))
            dve.tensor_copy(flag[0:1, 0:1], flag_f).then_inc(flag_ready, 1)
            dve.wait_ge(flag_spread, 1)
            link(dve.tensor_copy(flag_all, bank[5][:, 0:1]))
            link(dve.scalar_tensor_tensor(out=rel_groups, in0=spread(first_bc, 2, 2), scalar=flag_all,
                                          in1=rel_groups, op0=ALU.mult, op1=ALU.add))
            dve.wait_ge(weights_landed, 16 * len(placed))
            for tile, factor in scaled:
                dve.tensor_scalar(tile, tile, factor, None, ALU.mult).then_inc(weights_scaled, 1)
            dve.wait_ge(comp_ready, 1)
            g = c1 * C_X
            dve.tensor_scalar(comp[0:64, :], bank[4][0:64, 0:192], g, None, ALU.mult).then_inc(comp_scaled, 1)
            dve.tensor_scalar(comp[64:96, 0:128], bank[4][64:96, 0:128], g * INV_SQRT(3), None,
                              ALU.mult).then_inc(comp_scaled, 1)
            dve.tensor_scalar(comp[64:96, 128:192], bank[4][64:96, 128:192], g, None,
                              ALU.mult).then_inc(comp_scaled, 1)
            dve.memset(acc[:, 0:SCRATCH], 0.0).then_inc(acc_zeroed, 1)

            def rows0(j):
                dve.wait_ge(n0_mm, j + 1)
                wait(dve, n0_stored, 16 * j)
                dve.tensor_tensor(h_out, half[0][:, :, 0:D], spread(coef_of(0), 2, D), ALU.mult).then_inc(n0_out, 1)

            looped(dve, n_steps, rows0)
            dve.wait_ge(n0_stored, 16 * n_steps)
            dve.wait_ge(comp_placed, 16 * len(comp_parts))
            dve.wait_ge(acc_zeroed, 2)
            branched(dve, edge_vector, 0, L0)

            def rows1(j):
                link = Link(dve, chain[0], j * LINKS1)
                dve.wait_ge(n1_in, LOADS1 * j + LOADS1)
                dve.wait_ge(n1_tile, NB * j + NB)
                dve.tensor_tensor(pre, half[0][:, :, 0:192], spread(coef_of(0), 2, 192),
                                  ALU.mult).then_inc(n1_scaled, 1)
                dve.wait_ge(n1_scaled, j + 1)
                dve.wait_ge(n1_gates, j + 1)
                link(dve.tensor_tensor(z[:, :, 0:S], pre[:, :, 0:S], gates[:, :, 0:S], ALU.mult))
                link(dve.tensor_tensor(
                    z[:, :, S:D].rearrange("p t (i c) -> p t i c", i=3),
                    pre[:, :, 96:192].rearrange("p t (i c) -> p t i c", i=3),
                    spread(gates[:, :, S:96], 2, 3), ALU.mult))
                link(dve.tensor_tensor(z, z, x_rows, ALU.add))
                norm(dve, 0, j, link)
                dve.tensor_tensor(z, z, spread(stat[:, 0], 2, D), ALU.mult).then_inc(n1_x1, 1)
                dve.wait_ge(n1_x1, j + 1)
                for t in range(NB):
                    c = j * NB + t
                    dve.wait_ge(n1_h_mm, c + 1)
                    link(dve.tensor_scalar(h_out[:, t], bank[6][:, D:2 * D], coef[:, 1, t:t + 1], None, ALU.mult))
                    dve.scalar_tensor_tensor(out=h_out[:, t], in0=bank[6][:, 0:D], scalar=coef[:, 0, t:t + 1],
                                             in1=h_out[:, t], op0=ALU.mult, op1=ALU.add).then_inc(n1_h_used, 1)
                    dve.wait_ge(n1_self_mm, c + 1)
                    link(dve.scalar_tensor_tensor(out=x_rows[:, t], in0=bank[7][:, 0:D],
                                                  scalar=coef[:, 0, t:t + 1], in1=z[:, t], op0=ALU.mult,
                                                  op1=ALU.add))
                    dve.scalar_tensor_tensor(out=x_rows[:, t], in0=bank[7][:, D:2 * D], scalar=coef[:, 1, t:t + 1],
                                             in1=x_rows[:, t], op0=ALU.mult, op1=ALU.add).then_inc(n1_self_used, 1)
                assert link.n == LINKS1, link.n

            looped(dve, n_steps, rows1)
            dve.wait_ge(n1_stored, 32 * n_steps)
            dve.wait_ge(acc_zeroed, 2 + zero_parts)
            branched(dve, edge_vector, 1, L1)

            def rows2(j):
                link = Link(dve, chain[1], j * LINKS2)
                dve.wait_ge(n2_in, LOADS2 * j + LOADS2)
                dve.tensor_tensor(am[:, 0], coef[:, 0], coef[:, 2], ALU.mult)
                link(dve.tensor_tensor(am[:, 1], coef[:, 1], coef[:, 2], ALU.mult))
                dve.wait_ge(n2_tile, NB * j + NB)
                wait(dve, n2_stored, 16 * j)
                o = ps[:, 0:NB * 512].rearrange("p (t c) -> p t c", t=NB)
                dve.tensor_tensor(z, o[:, :, 0:D], spread(am[:, 0], 2, D), ALU.mult).then_inc(n2_scaled, 1)
                dve.tensor_tensor(h_out, o[:, :, D:2 * D], spread(am[:, 1], 2, D), ALU.mult).then_inc(n2_scaled, 1)
                dve.wait_ge(n2_scaled, 2 * j + 2)
                link(dve.tensor_tensor(z, z, h_out, ALU.add))
                link(dve.tensor_tensor(z, z, x_rows, ALU.add))
                norm(dve, 1, j, link)
                dve.tensor_tensor(h_out[:, :, 0:S], z[:, :, 0:S], spread(stat[:, 0], 2, S),
                                  ALU.mult).then_inc(n2_out, 1)
                dve.tensor_tensor(h_out[:, :, S:D].rearrange("p t (c i) -> p t i c", i=3),
                                  z[:, :, S:D].rearrange("p t (i c) -> p t i c", i=3),
                                  spread(spread(stat[:, 0], 2, 3), 3, V), ALU.mult).then_inc(n2_out, 1)
                assert link.n == LINKS2, link.n

            looped(dve, n_steps, rows2)


def kernel(x, src, dst, edge_attr_10, edge_attr_4, edge_attr_64, node_vec1, node_vec1_n2, node_vec1_n3, **weights):
    import numpy as np
    import concourse.bacc as bacc
    from concourse.bass_utils import run_bass_kernel_spmd

    x, src, dst = np.asarray(x), np.asarray(src), np.asarray(dst)
    n, e = x.shape[0], src.shape[0]
    n_iter = -(-e // ITER)
    e_pad = n_iter * ITER
    n_steps = -(-n // (NB * P))
    n_pad = n_steps * NB * P

    def pad(a, rows, **kw):
        a = np.asarray(a)
        return np.pad(a, [(0, rows - a.shape[0])] + [(0, 0)] * (a.ndim - 1), **kw)

    def by_tile(a):
        return np.ascontiguousarray(np.moveaxis(a.reshape(-1, TILE, *a.shape[1:]), 0, 1))

    xp = pad(x, n_pad)
    x_rows = np.concatenate([xp[:, :S], xp[:, S:].reshape(n_pad, V, 3).transpose(0, 2, 1).reshape(n_pad, 3 * V)], 1)
    turned = x_rows.reshape(n_steps, NB * P, D).transpose(0, 2, 1)
    coef = np.concatenate([pad(a, n_pad) for a in (node_vec1, node_vec1_n2, node_vec1_n3)], 1)
    dst_p = pad(dst, e_pad, mode="edge")
    e64 = pad(edge_attr_64, e_pad).reshape(n_iter, Q, 2, TILE, 64)
    arrays = {
        "x_rows": x_rows,
        "xs": turned[:, :S], "xv": turned[:, S:],
        "coef": coef.reshape(n_steps, NB, P, 3).transpose(0, 2, 3, 1),
        "src": by_tile(pad(src, e_pad)), "dst": by_tile(dst_p), "first": dst_p[::GROUP][None],
        "attr": by_tile(pad(edge_attr_4, e_pad)),
        "edge64": e64.transpose(0, 2, 4, 1, 3).reshape(n_iter, P, ITER // 2),
        "edge10": pad(edge_attr_10, e_pad).reshape(n_iter, ITER, 10).transpose(0, 2, 1),
        "iota": np.tile(np.arange(WIN, dtype=np.float32), (P, 1)),
        "ident": np.eye(P, dtype=np.float32),
    }
    for name, w in weights.items():
        w = np.asarray(w)
        if name[-6:] in ("s_l2_a", "s_l2_c", "v_l2_a", "v_l2_c"):
            arrays[name[-7:] + "_t"] = w.T
        else:
            arrays[name] = w

    nc = bacc.Bacc("TRN2", target_bir_lowering=False, num_devices=1)
    arrays = {k: np.ascontiguousarray(a) for k, a in arrays.items()}
    ins = {k: nc.dram_tensor(f"in_{k}", a.shape, mybir.dt.from_np(a.dtype), kind="ExternalInput").ap()
           for k, a in arrays.items()}
    out = nc.dram_tensor("out", (n_pad, D), F32, kind="ExternalOutput").ap()
    gnn_kernel(nc, ins, out, n, e)
    r = run_bass_kernel_spmd(nc, [{f"in_{k}": a for k, a in arrays.items()}], core_ids=[0])
    return r.results[0]["out"][:n]
```

```python
import math
from contextlib import ExitStack

import concourse.bass as bass
from concourse import mybir
from concourse.alu_op_type import AluOpType as ALU

F32 = mybir.dt.float32
I32 = mybir.dt.int32
ACT = mybir.ActivationFunctionType
AX = mybir.AxisListType

P = 128
TILE = 128
GROUP = 2 * TILE
Q = 4
ITER = Q * GROUP
PAIR = 2 * GROUP
WIN = 32
NB = 5
S, V = 64, 32
D = S + 3 * V
EPS = 1e-5
INV_SQRT = lambda d: 1.0 / float(d) ** 0.5


class Layer:

    def __init__(self, vector_products, hidden, chunks):
        self.k = vector_products
        self.wn = 2 * S + V * self.k
        self.hidden = hidden
        self.pn = 2 * S + 3 * V * self.k
        self.chunks = chunks
        self.units = sum(len(range(4)[c[2]]) for c in chunks)


def iterations(n_edges):
    return -(-n_edges // ITER) | 1


def gnn_kernel(nc, ins, out, n_nodes, n_edges):
    n_iter = iterations(n_edges)
    n_groups = n_iter * Q
    n_pairs = n_groups // 2
    n_tiles = 2 * n_groups
    n_steps = -(-n_nodes // (NB * P))
    n_pad = n_steps * NB * P
    n_win = -(-n_nodes // WIN)
    assert n_iter >= 4 and n_nodes + WIN - 1 <= n_pad

    L0 = Layer(3, 64, [(S, P, slice(1, 4), 0), (S + P, P, slice(1, 4), 3), (S + 2 * P, 96, slice(0, 1), 6),
                       (0, S, slice(0, 1), 7)])
    L1 = Layer(2, 100, [(S, P, slice(1, 4), 0), (S + P, P, slice(0, 4, 3), 3), (0, S, slice(0, 1), 5)])
    U0, U1 = L0.units, L1.units

    R0A, R0B, R0C, R0D = 0, 3 * 96, 3 * 96 + 3 * 192, 4 * 96 + 3 * 192
    R0_COLS = R0D + 96
    R1S, R1V, R1W = 0, 4 * 128, 4 * 128 + 192
    R1_COLS = R1W + 64

    with ExitStack() as ctx:
        def sb(name, shape, dt=F32):
            return ctx.enter_context(nc.sbuf_tensor(name, shape, dt))

        def sem(name):
            return ctx.enter_context(nc.semaphore(name))

        acc = sb("acc", [P, n_pad * U0])
        attr = sb("attr", [P, n_tiles, 4])
        rel = sb("rel", [P, n_pairs, 4])
        first = sb("first", [P, n_pairs], I32)
        flag = sb("flag", [P, 8], I32)
        iota = sb("iota", [P, WIN])
        window = sb("window", [P, WIN])
        ident = sb("ident", [P, P])
        w1_0 = sb("w1_0", [P, P])
        w2_0 = sb("w2_0", [P, L0.wn])
        w1_1 = sb("w1_1", [P, P])
        w2_1 = sb("w2_1", [P, L1.wn])
        lin0 = sb("lin0", [P, 2 * 96])
        self0 = sb("self0", [P, 2 * 96])
        lin1s = sb("lin1s", [P, 4 * S])
        lin1v = sb("lin1v", [P, 4 * 96])
        r0 = sb("r0", [P, R0_COLS])
        r1 = sb("r1", [P, R1_COLS])
        edge_in = sb("edge_in", [P, ITER])
        hidden = sb("hidden", [P, ITER])
        idx = sb("idx", [P, 2, 2 * Q], I32)
        prod = sb("prod", [P, Q, 2, L0.pn])
        rows = sb("rows", [P, Q, 2, D])
        hot = sb("hot", [P, 2, 4, WIN])
        whot = sb("whot", [P, 2, 4, WIN, 4])
        stage = sb("stage", [P, U0 * P])
        xs = sb("xs", [S, NB, P])[:]
        xv = sb("xv", [96, NB, P])[:]
        xs_flat, xv_flat = (a.rearrange("p t n -> p (t n)") for a in (xs, xv))
        x_rows = sb("x_rows", [P, NB, D])[:]
        z = sb("z", [P, NB, D])[:]
        pre = sb("pre", [P, NB, 192])[:]
        h_out = pre[:, :, 0:D]
        gates = sb("gates", [P, NB, 96])
        coef = sb("coef", [P, 4, NB])
        am = sb("am", [P, 2, NB])
        stat = sb("stat", [P, 4, NB])
        eps = sb("eps", [P, 1])


        ps = ctx.enter_context(nc.psum_tensor("ps", [P, 8 * 512], F32))
        bank = [ps[:, 512 * b:512 * b + 512] for b in range(8)]
        hid_ps = ps[:, 0:2 * 512]
        half = [ps[:, 512 * b:512 * b + NB * 256].rearrange("p (t c) -> p t c", t=NB) for b in (0, 3)]

        h_dram = [nc.dram_tensor(f"h{l}_rows", [n_pad, D], F32).ap() for l in range(2)]
        base_dram = nc.dram_tensor("base_rows", [n_pad, D], F32).ap()

        loaded = sem("loaded")
        cleared = sem("cleared")
        weights_landed = sem("weights_landed")
        weights_scaled = sem("weights_scaled")
        first_cast = sem("first_cast")
        first_spread = sem("first_spread")
        setup_step = sem("setup_step")
        far_found = sem("far_found")
        far_turned = sem("far_turned")
        flag_ready = sem("flag_ready")
        flag_spread = sem("flag_spread")
        comp_ready = sem("comp_ready")
        comp_scaled = sem("comp_scaled")
        comp_placed = sem("comp_placed")
        acc_zeroed = sem("acc_zeroed")
        banks_cleared = sem("banks_cleared")
        edges_done = [sem(f"edges_done{l}") for l in range(2)]
        n0_in, n0_mm, n0_out, n0_stored = sem("n0_in"), sem("n0_mm"), sem("n0_out"), sem("n0_stored")
        n1_in, n1_staged, n1_tile = sem("n1_in"), sem("n1_staged"), sem("n1_tile")
        n1_scaled, n1_gates, n1_x1 = sem("n1_scaled"), sem("n1_gates"), sem("n1_x1")
        n1_turned, n1_copied = sem("n1_turned"), sem("n1_copied")
        n1_h_mm, n1_h_used, n1_self_mm, n1_self_used = (sem("n1_h_mm"), sem("n1_h_used"), sem("n1_self_mm"),
                                                        sem("n1_self_used"))
        n1_stored = sem("n1_stored")
        n2_in, n2_staged, n2_tile, n2_scaled = sem("n2_in"), sem("n2_staged"), sem("n2_tile"), sem("n2_scaled")
        n2_out, n2_stored = sem("n2_out"), sem("n2_stored")
        chain = [sem("n1_chain"), sem("n2_chain")]
        var_ready = [sem("n1_var"), sem("n2_var")]
        std_ready = [sem("n1_std"), sem("n2_std")]

        passed = sem("passed")

        block = ctx.enter_context(nc.Block())

        def wait(eng, s, value):
            if not isinstance(value, int) or value > 0:
                eng.wait_ge(s, value)

        def hold(eng, s, value):
            if not isinstance(value, int) or value > 0:
                eng.wait_ge(s, value)
                eng.sem_inc(passed, 1)

        def looped2(eng, body):
            body(0, 0)
            with eng.Fori(1, n_iter - 1, 2) as i:
                body(i, 1)
                body(i + 1, 0)

        def looped(eng, count, body, first=1, peel_last=False):
            for i in range(first):
                body(i)
            end = count - 1 if peel_last else count
            if end > first:
                with eng.Fori(first, end) as i:
                    body(i)
            if peel_last:
                body(count - 1)

        def spread(ap, axis, n):
            ap = ap.unsqueeze(axis)
            shape = list(ap.shape)
            shape[axis] = n
            return ap.to_broadcast(shape)

        fc1, fc2 = ins["L0_gnn_fc_w1"], ins["L0_gnn_fc_w2"]
        placed = [(w1_0[0:64, 0:64], fc1), (w1_0[64:128, 64:128], fc1)]
        for o, a, b in ((0, 0, 128), (128, 192, 224), (160, 160, 192), (192, 128, 160)):
            placed += [(w2_0[p:p + 64, o:o + b - a], fc2[:, a:b]) for p in (0, 64)]
        for o, a, b in ((0, 0, 128), (128, 160, 192), (160, 128, 160)):
            placed.append((w2_1[0:100, o:o + b - a], ins["L1_gnn_W_fc2"][:, a:b]))
        placed += [(w1_1[p:p + 10, 0:100], ins["L1_gnn_W_fc1"]) for p in (0, 32)]
        lin2s, lin2v = ins["L0_gnn_lin2_ws"], ins["L0_gnn_lin2_wv"]
        placed += [
            (lin0[0:S, 0:S], ins["L0_gnn_lin1_ws"]), (self0[0:S, 0:96], ins["L0_gnn_sc_ws"]),
            (r0[0:S, R0D:R0D + 96], lin2s[0:64]),
        ]
        for i in range(3):
            placed += [
                (lin0[V * i:V * i + V, 96 + V * i:96 + V * i + V], ins["L0_gnn_lin1_wv"]),
                (self0[V * i:V * i + V, 96 + V * i:96 + V * i + V], ins["L0_gnn_sc_wv"]),
            ]
        for m, part in enumerate(("l1_a", "l1_c", "sc_a", "sc_c")):
            placed.append((lin1s[0:S, m * S:m * S + S], ins[f"L1_gnn_Ws_{part}"]))
            for i in range(3):
                placed.append((lin1v[V * i:V * i + V, m * 96 + V * i:m * 96 + V * i + V], ins[f"L1_gnn_Wv_{part}"]))
        signs = []
        for k in range(3):
            a, b = R0A + 96 * k, R0B + 192 * k
            placed.append((r0[0:64, a + V * k:a + V * k + V], lin2v[0:64]))
            placed.append((r0[V + V * k:2 * V + V * k, b:b + 96], lin2s[64:96]))
            placed.append((r0[V * k:V * k + V, R0C + V * k:R0C + V * k + V], lin2v[64:96]))
            for j, i, sign in (((k + 1) % 3, (k + 2) % 3, 1), ((k + 2) % 3, (k + 1) % 3, -1)):
                r, col = ((64, a), (96, a), (0, b + 96))[i]
                part = r0[r:r + V, col + V * j:col + V * j + V]
                placed.append((part, lin2v[96:128]))
                signs.append((part, sign))
        l2t, l3, comp = acc[0:96, 0:4 * 96], acc[0:96, 384:384 + 96], acc[0:96, 512:512 + 192]
        for m, part in enumerate(("Ws_l2_a_t", "Ws_l2_c_t", "Wv_l2_a_t", "Wv_l2_c_t")):
            placed.append((l2t[:, 96 * m:96 * m + 96], ins[part]))
        placed += [(l3[:, 0:S], ins["L1_gnn_Ws_l3"]), (l3[:, S:96], ins["L1_gnn_Wv_l3"])]
        comp_parts = [
            (r1[0:64, R1S:R1S + 128], comp[0:64, 0:128]),
            (r1[64:96, R1S + 128:R1S + 256], comp[64:96, 0:128]),
            (r1[96:128, R1S + 256:R1S + 384], comp[64:96, 0:128]),
            (r1[0:32, R1S + 384:R1S + 512], comp[64:96, 0:128]),
            (r1[0:64, R1W:R1W + 64], comp[0:64, 128:192]),
        ]
        for k in range(3):
            for m in range(2):
                col = R1V + 96 * m + V * k
                comp_parts.append((r1[V + V * k:2 * V + V * k, col:col + V], comp[64:96, 128 + V * m:128 + V * m + V]))

        setup = acc[:, 1024:]
        dst_i = setup[:, 0:n_tiles].bitcast(I32)
        dst_f = setup[:, n_tiles:2 * n_tiles]
        far = setup[:, 2 * n_tiles:3 * n_tiles]
        first_f = setup[0:1, 3 * n_tiles:3 * n_tiles + n_pairs]
        o = 3 * n_tiles + n_pairs
        far_max = setup[:, o:o + 1]
        far_row = setup[0:1, o + 1:o + 2]
        flag_f = setup[0:1, o + 2:o + 3]
        flag_all = setup[:, o + 3:o + 4]
        ones = setup[0:1, o + 4:o + 4 + P]
        SCRATCH = 1024 + o + 4 + P
        assert n_pairs <= 512 and SCRATCH <= n_pad * U1
        first_bc = bank[7][:, 0:n_pairs]

        tables = [(dst_i, ins["dst"]), (first[0:1, :], ins["first"]), (iota[:], ins["iota"]),
                  (ident[:], ins["ident"]), (attr[:], ins["attr"])]
        clears = [w1_0[:], w1_1[:], w2_1[:], lin0[:], self0[:], lin1v[:], r0[:], r1[:]]

        c0 = INV_SQRT(64) * INV_SQRT(16)
        c1 = INV_SQRT(16)
        C_S, C_X = math.sin(math.pi / 8.0), math.cos(math.pi / 8.0)
        scaled = [
            (lin0[0:S, 0:S], INV_SQRT(S)), (lin0[0:96, 96:192], INV_SQRT(V)),
            (self0[0:S, 0:96], INV_SQRT(S)), (self0[0:96, 96:192], INV_SQRT(V)),
            (r0[:, 0:R0B], c0 * INV_SQRT(128)),
            (r0[:, R0B:R0C].rearrange("p (k m c) -> p k m c", k=3, m=2)[:, :, 0], c0 * INV_SQRT(96) * INV_SQRT(3)),
            (r0[:, R0B:R0C].rearrange("p (k m c) -> p k m c", k=3, m=2)[:, :, 1], c0 * INV_SQRT(128)),
            (r0[:, R0C:R0D], c0 * INV_SQRT(128)), (r0[:, R0D:R0D + 96], c0 * INV_SQRT(96)),
            (lin1s[0:S, 2 * S:4 * S], C_S), (lin1v[0:96, 192:384], C_S),
        ]
        signed = [(part, sign * INV_SQRT(2)) for part, sign in signs]

        def at(ap, j):
            if isinstance(j, int):
                return ap[j]
            ap = ap[bass.ds(j, 1)]
            return ap.rearrange("o p c -> (o p) c" if len(ap.shape) == 3 else "o p t c -> (o p) t c")

        def step_rows(dram):
            return dram.rearrange("(j t p) c -> j p t c", t=NB, p=P)

        def coef_of(m):
            return coef[:, m]

        def stage_tiles(act, layer, staged, used, j):
            U = layer.units
            for t in range(NB):
                c = j * NB + t
                wait(act, used, c)
                s = acc[:, c * (U * P):(c + 1) * (U * P)] if isinstance(c, int) else \
                    acc[:, bass.ds(c * (U * P), U * P)]
                act.activation(stage[:, 0:U * P], s, ACT.Copy).then_inc(staged, 1)

        def unit(layer, u):
            return stage[:, 0:layer.units * P].rearrange("p (n u) -> p n u", u=layer.units)[:, :, u]

        def norm(dve, l, j, link):
            link(dve.tensor_reduce(stat[:, 0], z, AX.X, ALU.add))
            link(dve.tensor_scalar(stat[:, 1], stat[:, 0], 1.0 / D, None, ALU.mult))
            link(dve.tensor_tensor(z, z, spread(stat[:, 1], 2, D), ALU.subtract))
            link(dve.tensor_tensor(h_out, z, z, ALU.mult))
            dve.tensor_reduce(stat[:, 2], h_out, AX.X, ALU.add).then_inc(var_ready[l], 1)
            dve.wait_ge(std_ready[l], j + 1)
            link(dve.reciprocal(stat[:, 0], stat[:, 3]))

        def deviation(act, l, j):
            act.wait_ge(var_ready[l], j + 1)
            act.activation(stat[:, 3], stat[:, 2], ACT.Sqrt, bias=eps[:], scale=1.0 / D).then_inc(std_ready[l], 1)

        class Link:

            def __init__(self, eng, s, start):
                self.eng, self.s, self.start, self.n = eng, s, start, 0

            def __call__(self, ins_):
                self.n += 1
                ins_.then_inc(self.s, 1)
                self.eng.wait_ge(self.s, self.start + self.n)

        class Edge:
            def __init__(self, n):
                self.loaded = sem(f"e{n}_loaded")
                self.mixed = sem(f"e{n}_mixed")
                self.hidden = sem(f"e{n}_hidden")
                self.weights = sem(f"e{n}_weights")
                self.index = [sem(f"e{n}_index{p}") for p in range(2)]
                self.rows = [sem(f"e{n}_rows{q}") for q in range(Q)]
                self.hot = sem(f"e{n}_hot")
                self.whot = sem(f"e{n}_whot")
                self.prod = sem(f"e{n}_prod")
                self.agg = sem(f"e{n}_agg")
                self.added = sem(f"e{n}_added")
                self.window = sem(f"e{n}_window")

        edge = [Edge(0), Edge(1)]
        edge_feats = [ins["edge64"], ins["edge10"]]

        def edge_loads(sp, l):
            e = edge[l]
            used = P if l == 0 else 10
            cols = ITER // 2 if l == 0 else ITER

            def nodes(i, par):
                sp.dma_start(idx[:, par], at(ins["src"], i)).then_inc(e.index[par], 16)

            def features(i):
                s = at(edge_feats[l], i)
                if l == 0:
                    sp.dma_start(edge_in[:, 0:512], s).then_inc(e.loaded, 16)
                else:
                    sp.dma_start(edge_in[0:10, 0:512], s[0]).then_inc(e.loaded, 16)
                    sp.dma_start(edge_in[32:42, 0:512], s[1]).then_inc(e.loaded, 16)

            def body(i, par):
                hold(sp, e.mixed, i)
                features(i)
                for q in range(Q):
                    hold(sp, e.rows[q], 32 * i)
                nodes(i + 1, par)

            nodes(0, 0)
            nodes(1, 1)
            features(0)
            body(1, 0)
            with sp.Fori(2, n_iter - 2, 2) as i:
                body(i, 1)
                body(i + 1, 0)
            hold(sp, e.mixed, n_iter - 1)
            features(n_iter - 1)

        def edge_gathers(pool, l):
            e = edge[l]

            def body(i, par):
                hold(pool, e.index[par], 8 * i + 16 - 8 * par)
                for q in range(Q):
                    hold(pool, e.prod, i * Q + q - Q + 1)
                    for h in range(2):
                        pool.indirect_dma_start(
                            out=rows[:, q, h], out_offset=None, in_=h_dram[l],
                            in_offset=bass.IndirectOffsetOnAxis(ap=idx[:, par, 2 * q + h:2 * q + h + 1], axis=0),
                        ).then_inc(e.rows[q], 16)

            looped2(pool, body)

        def edge_silu(act, l):
            e = edge[l]
            wide = P if l == 0 else GROUP
            scale = INV_SQRT(64) if l == 0 else 1.0

            def body(i):
                act.wait_ge(e.mixed, i + 1)
                for q in range(Q):
                    wait(act, e.weights, (i - 1) * Q + q + 1)
                    act.activation(hidden[:, q * wide:(q + 1) * wide], hid_ps[:, q * wide:(q + 1) * wide], ACT.Silu,
                                   scale=scale).then_inc(e.hidden, 1)

            looped(act, n_iter, body)

        def weights_of(q):
            b = 2 + 4 * (q % 2)
            return ps[:, 512 * b:512 * b + 1024].rearrange("p (h c) -> p h c", h=2)

        def edge_tensor(pe, l, layer, general):
            e = edge[l]
            lag = 0 if general else 2
            loads = 16 if l == 0 else 32

            def mix(i):
                pe.wait_ge(e.loaded, loads * i + loads)
                wait(pe, e.hidden, Q * i)
                if l == 0:
                    pe.matmul(bank[0], w1_0[:], edge_in[:, 0:512], start=True, stop=True).then_inc(e.mixed, 1)
                else:
                    pe.matmul(bank[0], w1_1[0:10], edge_in[0:10, 0:512], start=True, stop=True)
                    pe.matmul(bank[1], w1_1[32:42], edge_in[32:42, 0:512], start=True,
                              stop=True).then_inc(e.mixed, 1)

            def radial(i, q):
                pe.wait_ge(e.hidden, i * Q + q + 1)
                wait(pe, e.prod, i * Q + q - 1)
                w = weights_of(q)
                for h in range(2):
                    if l == 0:
                        r = slice(64 * h, 64 * h + 64)
                        mm = pe.matmul(w[:, h, 0:layer.wn], hidden[r, q * P:(q + 1) * P], w2_0[r], start=True,
                                       stop=True)
                    else:
                        c = (2 * q + h) * P
                        mm = pe.matmul(w[:, h, 0:layer.wn], hidden[:, c:c + P], w2_1[:], start=True, stop=True)
                mm.then_inc(e.weights, 1)

            def sums(q, slot):
                o = bank[4 + slot][:, 0:WIN * layer.units].rearrange("p (n u) -> p n u", u=layer.units)
                for h in range(2):
                    t = 2 * (q % 2) + h
                    for m, (c, size, attrs, u) in enumerate(layer.chunks):
                        count = len(range(4)[attrs])
                        mm = pe.matmul(o[0:size, :, u:u + count], prod[:, q, h, c:c + size],
                                       whot[:, slot, t, :, attrs], start=(t == 0 and m == 0),
                                       stop=(t == 3 and m == len(layer.chunks) - 1), skip_group_check=True)
                mm.then_inc(e.agg, 1)

            def lagged(i, q):
                n = i * Q + q - lag
                if isinstance(n, int) and n < 0:
                    return
                m = (q - lag) % Q
                if m % 2 == 0:
                    pe.wait_ge(e.whot, (i * Q + q - lag - m) // 2 + m // 2 + 1 if isinstance(i, int)
                               else i * 2 + (q - lag + 1) // 2 + 1)
                    w = (n // 2 - 1) if isinstance(i, int) else i * 2 + (q - lag) // 2 - 1
                    wait(pe, e.added, w)
                pe.wait_ge(e.prod, n + 1)
                sums(m, m // 2)

            def body(i, last=False):
                for q in range(Q):
                    radial(i, q)
                    if q == 1 and not last:
                        mix(i + 1)
                    if not general:
                        lagged(i, q)
                    elif q % 2 == 1:
                        w = i * 2 + q // 2
                        hold(pe, e.prod, i * Q + q + 1)
                        with pe.Fori(0, n_win) as v:
                            pe.wait_ge(e.whot, w * n_win + v + 1)
                            sums(q - 1, 0)
                            sums(q, 0)

            pe.wait_ge(banks_cleared, l + 1)
            mix(0)
            looped(pe, n_iter - 1, body, first=2)
            body(n_iter - 1, last=True)
            if not general:
                for q in range(lag):
                    lagged(n_iter, q)

        def edge_vector(dve, l, layer, general):
            e = edge[l]
            U = layer.units

            def weighted_hot(w, slot, hot_slot, count, nodes):
                r = rel[:, w] if isinstance(w, int) else rel[:, bass.ds(w, 1)].rearrange("p o t -> p (o t)")
                dve.tensor_tensor(hot[:, hot_slot], spread(nodes, 1, 4), spread(r, 2, WIN),
                                  ALU.is_equal).then_inc(e.hot, 1)
                dve.wait_ge(e.hot, count + 1)
                a = attr[:, 4 * w:4 * w + 4] if isinstance(w, int) else attr[:, bass.ds(w * 4, 4)]
                dve.tensor_tensor(whot[:, slot], spread(hot[:, hot_slot], 3, 4), spread(a, 2, WIN),
                                  ALU.mult).then_inc(e.whot, 1)

            def products(i, q):
                dve.wait_ge(e.rows[q], 32 * i + 32)
                dve.wait_ge(e.weights, i * Q + q + 1)
                w = weights_of(q)
                dve.tensor_tensor(prod[:, q, :, 0:2 * S].rearrange("p h (k c) -> p h k c", k=2),
                                  w[:, :, 0:2 * S].rearrange("p h (k c) -> p h k c", k=2),
                                  spread(rows[:, q, :, 0:S], 2, 2), ALU.mult)
                for h in range(2):
                    ins_ = dve.tensor_tensor(
                        prod[:, q, h, 2 * S:layer.pn].rearrange("p (k i c) -> p k i c", k=layer.k, i=3),
                        spread(w[:, h, 2 * S:layer.wn].rearrange("p (k c) -> p k c", k=layer.k), 2, 3),
                        spread(rows[:, q, h, S:D].rearrange("p (i c) -> p i c", i=3), 1, layer.k), ALU.mult)
                ins_.then_inc(e.prod, 1)

            def add(w, slot):
                s = first[0:1, w:w + 1] if isinstance(w, int) else first[0:1, bass.ds(w, 1)]
                offset = dve.value_load(s, min_val=0, max_val=n_nodes - 1) * U
                dve.wait_ge(e.agg, 2 * w + 2)
                wait(dve, e.added, w)
                a = acc[:, bass.ds(offset, WIN * U)]
                dve.tensor_tensor(a, a, bank[4 + slot][:, 0:WIN * U], ALU.add).then_inc(e.added, 1)

            def body(i):
                for slot in range(2):
                    w = i * 2 + slot
                    if not general:
                        wait(dve, e.agg, i * Q + 2 * slot - 2)
                        weighted_hot(w, slot, slot, w, iota[:])
                        products(i, 2 * slot)
                        if not isinstance(i, int) or i > 0:
                            add(w - 2, slot)
                        products(i, 2 * slot + 1)
                        continue
                    products(i, 2 * slot)
                    products(i, 2 * slot + 1)
                    dve.tensor_copy(window[:], iota[:]).then_inc(e.window, 1)
                    hold(dve, e.window, w * (n_win + 1) + 1)
                    with dve.Fori(0, n_win) as v:
                        count = w * n_win + v
                        weighted_hot(w, 0, 0, count, window[:])
                        dve.wait_ge(e.agg, count * 2 + 2)
                        a = acc[:, bass.ds(v * (WIN * U), WIN * U)]
                        dve.tensor_tensor(a, a, bank[4][:, 0:WIN * U], ALU.add).then_inc(e.added, 1)
                        dve.wait_ge(e.added, count + 1)
                        dve.tensor_scalar(window[:], window[:], float(WIN), None, ALU.add).then_inc(e.window, 1)
                        dve.wait_ge(e.window, w * (n_win + 1) + v + 2)

            dve.memset(ps[:, 4 * 512:6 * 512], 0.0).then_inc(banks_cleared, 1)
            looped(dve, n_iter, body, first=2)
            if not general:
                for slot in range(2):
                    add(n_pairs - 2 + slot, slot)
                dve.wait_ge(e.added, n_pairs)
            dve.sem_inc(edges_done[l], 1)

        LOADS0, LOADS1, LOADS2 = 3 * 16, 4 * 16, 2 * 16
        LINKS1, LINKS2 = 8 + 2 * NB, 8

        @block.sync
        def _(sp):
            for tile, s in tables:
                sp.dma_start(tile, s).then_inc(loaded, 16)
            sp.wait_ge(cleared, len(clears))
            for tile, s in placed:
                sp.dma_start(tile, s).then_inc(weights_landed, 16)

            def rows0(j):
                hold(sp, n0_out, j)
                sp.dma_start(xs_flat, at(ins["xs"], j)).then_inc(n0_in, 16)
                sp.dma_start(xv_flat, at(ins["xv"], j)).then_inc(n0_in, 16)
                sp.dma_start(coef[:, 0:3], at(ins["coef"], j)).then_inc(n0_in, 16)
                hold(sp, n0_out, j + 1)
                sp.dma_start(at(step_rows(h_dram[0]), j), h_out).then_inc(n0_stored, 16)

            looped(sp, n_steps, rows0)
            sp.wait_ge(comp_scaled, 3)
            for tile, s in comp_parts:
                sp.dma_start(tile, s).then_inc(comp_placed, 16)
            edge_loads(sp, 0)

            sp.wait_ge(edges_done[0], 1)
            sp.wait_ge(comp_placed, 16 * len(comp_parts))

            def rows1(j):
                sp.dma_start(xs_flat, at(ins["xs"], j)).then_inc(n1_in, 16)
                sp.dma_start(xv_flat, at(ins["xv"], j)).then_inc(n1_in, 16)
                sp.dma_start(coef[:, 0:3], at(ins["coef"], j)).then_inc(n1_in, 16)
                sp.dma_start(x_rows, at(step_rows(ins["x_rows"]), j)).then_inc(n1_in, 16)
                hold(sp, n1_h_used, NB * j + NB)
                hold(sp, n1_self_used, NB * j + NB)
                sp.dma_start(at(step_rows(h_dram[1]), j), h_out).then_inc(n1_stored, 16)
                sp.dma_start(at(step_rows(base_dram), j), x_rows).then_inc(n1_stored, 16)
                hold(sp, n1_stored, 32 * j + 32)

            looped(sp, n_steps, rows1)
            edge_loads(sp, 1)

            sp.wait_ge(edges_done[1], 1)

            def rows2(j):
                sp.dma_start(coef[:, 0:3], at(ins["coef"], j)).then_inc(n2_in, 16)
                sp.dma_start(x_rows, at(step_rows(base_dram), j)).then_inc(n2_in, 16)
                hold(sp, n2_out, 2 * j + 2)
                sp.dma_start(at(step_rows(out), j), h_out).then_inc(n2_stored, 16)

            looped(sp, n_steps, rows2)
            sp.wait_ge(n2_stored, 16 * n_steps)

        @block.gpsimd
        def _(pool):
            pool.memset(acc[:, SCRATCH:], 0.0).then_inc(acc_zeroed, 1)
            pool.wait_ge(n0_stored, 16 * n_steps)
            edge_gathers(pool, 0)
            cols = n_pad * U1
            a = 0
            for t in range(n_steps):
                b = min((t + 1) * NB * P * U0, cols)
                pool.wait_ge(n1_staged, NB * (t + 1))
                if a < b:
                    pool.memset(acc[:, a:b], 0.0).then_inc(acc_zeroed, 1)
                a = max(a, b)
            pool.wait_ge(n1_stored, 32 * n_steps)
            edge_gathers(pool, 1)

        zero_parts = len([t for t in range(n_steps) if t * NB * P * U0 < n_pad * U1])

        @block.scalar
        def _(act):
            edge_silu(act, 0)
            act.wait_ge(edges_done[0], 1)

            def step1(j):
                stage_tiles(act, L0, n1_staged, n1_tile, j)
                act.wait_ge(n1_scaled, j + 1)
                act.activation(gates[:], pre[:, :, 0:96], ACT.Sigmoid).then_inc(n1_gates, 1)
                deviation(act, 0, j)
                act.wait_ge(n1_turned, j + 1)
                act.activation(xs, half[1][0:S, :, 0:P], ACT.Copy).then_inc(n1_copied, 1)
                act.activation(xv, half[1][0:96, :, P:2 * P], ACT.Copy).then_inc(n1_copied, 1)

            looped(act, n_steps, step1)
            edge_silu(act, 1)
            act.wait_ge(edges_done[1], 1)

            def step2(j):
                stage_tiles(act, L1, n2_staged, n2_tile, j)
                deviation(act, 1, j)

            looped(act, n_steps, step2)

        def branched(eng, edges, l, layer):
            eng.wait_ge(flag_ready, 1)
            far_flag = eng.value_load(flag[0:1, 0:1], min_val=0, max_val=1)
            with eng.If(far_flag < 1):
                edges(eng, l, layer, False)
            with eng.Else():
                edges(eng, l, layer, True)

        @block.tensor
        def _(pe):
            pe.wait_ge(first_cast, 2)
            pe.matmul(first_bc, ones, first_f, start=True, stop=True).then_inc(first_spread, 1)
            pe.wait_ge(far_found, 1)
            pe.wait_ge(loaded, 16 * len(tables))
            pe.matmul(bank[6][0:1, 0:P], far_max, ident[:], start=True, stop=True).then_inc(far_turned, 1)
            pe.wait_ge(flag_ready, 1)
            pe.matmul(bank[5][:, 0:1], ones, flag_f, start=True, stop=True).then_inc(flag_spread, 1)
            pe.wait_ge(weights_landed, 16 * len(placed))
            for m in range(4):
                a, b = ((0, S), (0, S), (S, 96), (S, 96))[m]
                c = (0, 64, 128, 160)[m]
                mm = pe.matmul(bank[4][0:96, c:c + b - a], l2t[:, 96 * m:96 * m + 96], l3[:, a:b], start=True,
                               stop=True)
            mm.then_inc(comp_ready, 1)
            pe.wait_ge(weights_scaled, len(scaled) + len(signed))

            def rows0(j):
                pe.wait_ge(n0_in, LOADS0 * j + LOADS0)
                wait(pe, n0_out, j)
                for t in range(NB):
                    pe.matmul(half[0][:, t, 0:S], xs[:, t], lin0[0:S, 0:S], start=True, stop=True)
                    mm = pe.matmul(half[0][:, t, S:D], xv[:, t], lin0[0:96, 96:192], start=True, stop=True)
                mm.then_inc(n0_mm, 1)

            looped(pe, n_steps, rows0)
            pe.wait_ge(n0_out, n_steps)
            branched(pe, edge_tensor, 0, L0)
            pe.wait_ge(edges_done[0], 1)

            def rows1(j):
                pe.wait_ge(n1_in, LOADS1 * j + LOADS1)
                wait(pe, n1_scaled, j)
                for t in range(NB):
                    c = j * NB + t
                    o = half[0][:, t]
                    pe.wait_ge(n1_staged, c + 1)
                    pe.matmul(o[:, 0:96], xs[:, t], self0[0:S, 0:96], start=True, stop=False)
                    pe.matmul(o[:, 96:192], xv[:, t], self0[0:96, 96:192], start=False, stop=False,
                              skip_group_check=True)
                    for u in range(3):
                        pe.matmul(o[:, 96:192], unit(L0, u), r0[:, R0A + 96 * u:R0A + 96 * u + 96], start=False,
                                  stop=False, skip_group_check=True)
                    for u in range(3, 6):
                        b = R0B + 192 * (u - 3)
                        pe.matmul(o[:, 0:192], unit(L0, u), r0[:, b:b + 192], start=False, stop=False,
                                  skip_group_check=True)
                    pe.matmul(o[:, 96:192], unit(L0, 6)[0:96], r0[0:96, R0C:R0C + 96], start=False,
                              stop=True, skip_group_check=True)
                    pe.matmul(o[:, 0:96], unit(L0, 7)[0:S], r0[0:S, R0D:R0D + 96], start=False,
                              stop=True).then_inc(n1_tile, 1)
                pe.wait_ge(n1_x1, j + 1)
                for t in range(NB):
                    pe.transpose(half[1][0:96, t, P:2 * P], z[:, t, S:D], ident[:])
                    mm = pe.transpose(half[1][0:S, t, 0:P], z[:, t, 0:S], ident[:])
                mm.then_inc(n1_turned, 1)
                pe.wait_ge(n1_copied, 2 * j + 2)
                for t in range(NB):
                    c = j * NB + t
                    for m, used, done in ((0, n1_h_used, n1_h_mm), (1, n1_self_used, n1_self_mm)):
                        o = bank[6 + m][:, 0:2 * D].rearrange("p (m c) -> p m c", m=2)
                        wait(pe, used, c)
                        pe.matmul(o[:, :, 0:S], xs[:, t], lin1s[0:S, 2 * S * m:2 * S * m + 2 * S], start=True,
                                  stop=True)
                        pe.matmul(o[:, :, S:D], xv[:, t], lin1v[0:96, 192 * m:192 * m + 192], start=True,
                                  stop=True).then_inc(done, 1)

            looped(pe, n_steps, rows1)
            branched(pe, edge_tensor, 1, L1)
            pe.wait_ge(edges_done[1], 1)

            def rows2(j):
                wait(pe, n2_scaled, 2 * j)
                for t in range(NB):
                    pe.wait_ge(n2_staged, j * NB + t + 1)
                    o = bank[t][:, 0:2 * D].rearrange("p (m c) -> p m c", m=2)
                    for m, (u, k) in enumerate(((5, S), (0, P), (1, P), (4, 32))):
                        pe.matmul(o[:, :, 0:S], unit(L1, u)[0:k], r1[0:k, R1S + 128 * m:R1S + 128 * m + 128],
                                  start=(m == 0), stop=(m == 3))
                    pe.matmul(o[:, :, S:D], unit(L1, 3), r1[:, R1V:R1V + 192], start=True, stop=False)
                    for k in range(3):
                        mm = pe.matmul(o[:, :, S + V * k:S + V * k + V], unit(L1, k)[0:S], r1[0:S, R1W:R1W + 64],
                                       start=False, stop=(k == 2))
                    mm.then_inc(n2_tile, 1)

            looped(pe, n_steps, rows2)

        @block.vector
        def _(dve):
            for tile in clears:
                dve.memset(tile, 0.0).then_inc(cleared, 1)
            dve.memset(eps[:], EPS).then_inc(setup_step, 1)
            dve.memset(ones, 1.0).then_inc(first_cast, 1)
            dve.wait_ge(loaded, 16 * len(tables))
            link = Link(dve, setup_step, 1)
            dve.tensor_copy(first_f, first[0:1, :]).then_inc(first_cast, 1)
            link(dve.tensor_copy(dst_f, dst_i))
            dve.wait_ge(first_spread, 1)
            link(dve.tensor_tensor(rel[:], dst_f.rearrange("p (w t) -> p w t", t=4), spread(first_bc, 2, 4),
                                   ALU.subtract))
            middle = (WIN - 1) / 2
            link(dve.tensor_scalar(far, rel[:].rearrange("p w t -> p (w t)"), middle, None, ALU.subtract))
            link(dve.tensor_tensor(far, far, far, ALU.mult))
            dve.tensor_reduce(far_max, far, AX.X, ALU.max).then_inc(far_found, 1)
            dve.wait_ge(far_turned, 1)
            link(dve.tensor_reduce(far_row, bank[6][0:1, 0:P], AX.X, ALU.max))
            link(dve.tensor_scalar(flag_f, far_row, (middle + 0.5) ** 2, None, ALU.is_gt))
            dve.tensor_copy(flag[0:1, 0:1], flag_f).then_inc(flag_ready, 1)
            dve.wait_ge(flag_spread, 1)
            link(dve.tensor_copy(flag_all, bank[5][:, 0:1]))
            link(dve.scalar_tensor_tensor(out=rel[:], in0=spread(first_bc, 2, 4), scalar=flag_all,
                                          in1=rel[:], op0=ALU.mult, op1=ALU.add))
            dve.wait_ge(weights_landed, 16 * len(placed))
            for tile, factor in scaled:
                dve.tensor_scalar(tile, tile, factor, None, ALU.mult).then_inc(weights_scaled, 1)
            dve.wait_ge(weights_scaled, len(scaled))
            for tile, factor in signed:
                dve.tensor_scalar(tile, tile, factor, None, ALU.mult).then_inc(weights_scaled, 1)
            dve.wait_ge(comp_ready, 1)
            g = c1 * C_X
            dve.tensor_scalar(comp[0:64, :], bank[4][0:64, 0:192], g, None, ALU.mult).then_inc(comp_scaled, 1)
            dve.tensor_scalar(comp[64:96, 0:128], bank[4][64:96, 0:128], g * INV_SQRT(3), None,
                              ALU.mult).then_inc(comp_scaled, 1)
            dve.tensor_scalar(comp[64:96, 128:192], bank[4][64:96, 128:192], g, None,
                              ALU.mult).then_inc(comp_scaled, 1)
            def rows0(j):
                dve.wait_ge(n0_mm, j + 1)
                wait(dve, n0_stored, 16 * j)
                dve.tensor_tensor(h_out, half[0][:, :, 0:D], spread(coef_of(0), 2, D), ALU.mult).then_inc(n0_out, 1)

            looped(dve, n_steps, rows0)
            dve.wait_ge(n0_stored, 16 * n_steps)
            dve.wait_ge(comp_placed, 16 * len(comp_parts))
            dve.memset(acc[:, 0:SCRATCH], 0.0).then_inc(acc_zeroed, 1)
            dve.wait_ge(acc_zeroed, 2)
            branched(dve, edge_vector, 0, L0)

            def rows1(j):
                link = Link(dve, chain[0], j * LINKS1)
                dve.wait_ge(n1_in, LOADS1 * j + LOADS1)
                dve.wait_ge(n1_tile, NB * j + NB)
                dve.tensor_tensor(pre, half[0][:, :, 0:192], spread(coef_of(0), 2, 192),
                                  ALU.mult).then_inc(n1_scaled, 1)
                dve.wait_ge(n1_scaled, j + 1)
                dve.wait_ge(n1_gates, j + 1)
                link(dve.tensor_tensor(z[:, :, 0:S], pre[:, :, 0:S], gates[:, :, 0:S], ALU.mult))
                link(dve.tensor_tensor(
                    z[:, :, S:D].rearrange("p t (i c) -> p t i c", i=3),
                    pre[:, :, 96:192].rearrange("p t (i c) -> p t i c", i=3),
                    spread(gates[:, :, S:96], 2, 3), ALU.mult))
                link(dve.tensor_tensor(z, z, x_rows, ALU.add))
                norm(dve, 0, j, link)
                dve.tensor_tensor(z, z, spread(stat[:, 0], 2, D), ALU.mult).then_inc(n1_x1, 1)
                dve.wait_ge(n1_x1, j + 1)
                for t in range(NB):
                    c = j * NB + t
                    dve.wait_ge(n1_h_mm, c + 1)
                    link(dve.tensor_scalar(h_out[:, t], bank[6][:, D:2 * D], coef[:, 1, t:t + 1], None, ALU.mult))
                    dve.scalar_tensor_tensor(out=h_out[:, t], in0=bank[6][:, 0:D], scalar=coef[:, 0, t:t + 1],
                                             in1=h_out[:, t], op0=ALU.mult, op1=ALU.add).then_inc(n1_h_used, 1)
                    dve.wait_ge(n1_self_mm, c + 1)
                    link(dve.scalar_tensor_tensor(out=x_rows[:, t], in0=bank[7][:, 0:D],
                                                  scalar=coef[:, 0, t:t + 1], in1=z[:, t], op0=ALU.mult,
                                                  op1=ALU.add))
                    dve.scalar_tensor_tensor(out=x_rows[:, t], in0=bank[7][:, D:2 * D], scalar=coef[:, 1, t:t + 1],
                                             in1=x_rows[:, t], op0=ALU.mult, op1=ALU.add).then_inc(n1_self_used, 1)
                assert link.n == LINKS1, link.n

            looped(dve, n_steps, rows1)
            dve.wait_ge(n1_stored, 32 * n_steps)
            dve.wait_ge(acc_zeroed, 2 + zero_parts)
            branched(dve, edge_vector, 1, L1)

            def rows2(j):
                link = Link(dve, chain[1], j * LINKS2)
                dve.wait_ge(n2_in, LOADS2 * j + LOADS2)
                dve.tensor_tensor(am[:, 0], coef[:, 0], coef[:, 2], ALU.mult)
                link(dve.tensor_tensor(am[:, 1], coef[:, 1], coef[:, 2], ALU.mult))
                dve.wait_ge(n2_tile, NB * j + NB)
                wait(dve, n2_stored, 16 * j)
                o = ps[:, 0:NB * 512].rearrange("p (t c) -> p t c", t=NB)
                dve.tensor_tensor(z, o[:, :, 0:D], spread(am[:, 0], 2, D), ALU.mult).then_inc(n2_scaled, 1)
                dve.tensor_tensor(h_out, o[:, :, D:2 * D], spread(am[:, 1], 2, D), ALU.mult).then_inc(n2_scaled, 1)
                dve.wait_ge(n2_scaled, 2 * j + 2)
                link(dve.tensor_tensor(z, z, h_out, ALU.add))
                link(dve.tensor_tensor(z, z, x_rows, ALU.add))
                norm(dve, 1, j, link)
                dve.tensor_tensor(h_out[:, :, 0:S], z[:, :, 0:S], spread(stat[:, 0], 2, S),
                                  ALU.mult).then_inc(n2_out, 1)
                dve.tensor_tensor(h_out[:, :, S:D].rearrange("p t (c i) -> p t i c", i=3),
                                  z[:, :, S:D].rearrange("p t (i c) -> p t i c", i=3),
                                  spread(spread(stat[:, 0], 2, 3), 3, V), ALU.mult).then_inc(n2_out, 1)
                assert link.n == LINKS2, link.n

            looped(dve, n_steps, rows2)


def kernel(x, src, dst, edge_attr_10, edge_attr_4, edge_attr_64, node_vec1, node_vec1_n2, node_vec1_n3, **weights):
    import numpy as np
    import concourse.bacc as bacc
    from concourse.bass_utils import run_bass_kernel_spmd

    x, src, dst = np.asarray(x), np.asarray(src), np.asarray(dst)
    n, e = x.shape[0], src.shape[0]
    n_iter = iterations(e)
    e_pad = n_iter * ITER
    n_steps = -(-n // (NB * P))
    n_pad = n_steps * NB * P

    def pad(a, rows, **kw):
        a = np.asarray(a)
        return np.pad(a, [(0, rows - a.shape[0])] + [(0, 0)] * (a.ndim - 1), **kw)

    def by_tile(a):
        return np.ascontiguousarray(np.moveaxis(a.reshape(-1, TILE, *a.shape[1:]), 0, 1))

    xp = pad(x, n_pad)
    x_rows = np.concatenate([xp[:, :S], xp[:, S:].reshape(n_pad, V, 3).transpose(0, 2, 1).reshape(n_pad, 3 * V)], 1)
    turned = x_rows.reshape(n_steps, NB * P, D).transpose(0, 2, 1)
    coef = np.concatenate([pad(a, n_pad) for a in (node_vec1, node_vec1_n2, node_vec1_n3)], 1)
    dst_p = pad(dst, e_pad, mode="edge")
    e64 = pad(edge_attr_64, e_pad).reshape(n_iter, Q, 2, TILE, 64)
    arrays = {
        "x_rows": x_rows,
        "xs": turned[:, :S], "xv": turned[:, S:],
        "coef": coef.reshape(n_steps, NB, P, 3).transpose(0, 2, 3, 1),
        "src": pad(src, e_pad).reshape(n_iter, 2 * Q, TILE).transpose(0, 2, 1),
        "dst": by_tile(dst_p), "first": dst_p[::PAIR][None],
        "attr": by_tile(pad(edge_attr_4, e_pad)),
        "edge64": e64.transpose(0, 2, 4, 1, 3).reshape(n_iter, P, ITER // 2),
        "edge10": pad(edge_attr_10, e_pad).reshape(n_iter, 2, ITER // 2, 10).transpose(0, 1, 3, 2),
        "iota": np.tile(np.arange(WIN, dtype=np.float32), (P, 1)),
        "ident": np.eye(P, dtype=np.float32),
    }
    for name, w in weights.items():
        w = np.asarray(w)
        if name[-6:] in ("s_l2_a", "s_l2_c", "v_l2_a", "v_l2_c"):
            arrays[name[-7:] + "_t"] = w.T
        else:
            arrays[name] = w

    nc = bacc.Bacc("TRN2", target_bir_lowering=False, num_devices=1)
    arrays = {k: np.ascontiguousarray(a) for k, a in arrays.items()}
    ins = {k: nc.dram_tensor(f"in_{k}", a.shape, mybir.dt.from_np(a.dtype), kind="ExternalInput").ap()
           for k, a in arrays.items()}
    out = nc.dram_tensor("out", (n_pad, D), F32, kind="ExternalOutput").ap()
    gnn_kernel(nc, ins, out, n, e)
    r = run_bass_kernel_spmd(nc, [{f"in_{k}": a for k, a in arrays.items()}], core_ids=[0])
    return r.results[0]["out"][:n]
```

```python
import math
from contextlib import ExitStack

import concourse.bass as bass
from concourse import mybir
from concourse.alu_op_type import AluOpType as ALU

F32 = mybir.dt.float32
I32 = mybir.dt.int32
ACT = mybir.ActivationFunctionType
AX = mybir.AxisListType

P = 128
TILE = 128
GROUP = 2 * TILE
Q = 4
ITER = Q * GROUP
PAIR = 2 * GROUP
WIN = 32
NB = 5
S, V = 64, 32
D = S + 3 * V
EPS = 1e-5
INV_SQRT = lambda d: 1.0 / float(d) ** 0.5


class Layer:

    def __init__(self, vector_products, chunks):
        self.k = vector_products
        self.wn = 2 * S + V * self.k
        self.pn = 2 * S + 3 * V * self.k
        self.chunks = chunks
        self.units = sum(len(range(4)[c[2]]) for c in chunks)


R0A, R0B, R0C, R0D = 0, 3 * 96, 3 * 96 + 3 * 192, 4 * 96 + 3 * 192
R0_COLS = R0D + 96
R1S, R1V, R1W = 0, 4 * 128, 4 * 128 + 192
R1_COLS = R1W + 64

WEIGHTS = {
    "lin0": 2 * 96,
    "w1_0": P,
    "w2_0": 2 * S + 3 * V,
    "w1_1": P,
    "w2_1": 2 * S + 2 * V,
    "self0": 2 * 96,
    "lin1s": 2 * S,
    "lin1v": 4 * 96,
    "r0": R0_COLS,
    "l2t": 4 * 96,
    "l3": 96,
}


def cross_parts():
    parts = []
    for k in range(3):
        a, b = R0A + 96 * k, R0B + 192 * k + 96
        for j, i, sign in (((k + 1) % 3, (k + 2) % 3, 1), ((k + 2) % 3, (k + 1) % 3, -1)):
            row, col = ((64, a), (96, a), (0, b))[i]
            parts.append((row, col + V * j, sign))
    return parts


def iterations(n_edges):
    return -(-n_edges // ITER) | 1


def node_steps(n_nodes):
    return -(-n_nodes // (NB * P)) | 1


def gnn_kernel(nc, ins, out, n_nodes, n_edges):
    n_iter = iterations(n_edges)
    n_groups = n_iter * Q
    n_pairs = n_groups // 2
    n_tiles = 2 * n_groups
    n_steps = node_steps(n_nodes)
    n_pad = n_steps * NB * P
    n_win = -(-n_nodes // WIN)
    assert n_iter >= 4 and n_nodes + WIN - 1 <= n_pad

    L0 = Layer(3, [(S, P, slice(1, 4), 0), (S + P, P, slice(1, 4), 3), (S + 2 * P, 96, slice(0, 1), 6),
                   (0, S, slice(0, 1), 7)])
    L1 = Layer(2, [(S, P, slice(1, 4), 0), (S + P, P, slice(0, 4, 3), 3), (0, S, slice(0, 1), 5)])
    U0, U1 = L0.units, L1.units

    with ExitStack() as ctx:
        def sb(name, shape, dt=F32):
            return ctx.enter_context(nc.sbuf_tensor(name, shape, dt))

        def sem(name):
            return ctx.enter_context(nc.semaphore(name))

        acc = sb("acc", [P, n_pad * U0])
        attr = sb("attr", [P, n_tiles, 4])
        rel = sb("rel", [P, n_pairs, 4])
        first = sb("first", [P, n_pairs], I32)
        flag = sb("flag", [P, 8], I32)
        iota = sb("iota", [P, WIN])
        window = sb("window", [P, WIN])
        ident = sb("ident", [P, P])
        weights = sb("weights", [P, sum(WEIGHTS.values())])
        w, o = {}, 0
        for name, cols in WEIGHTS.items():
            w[name] = weights[:, o:o + cols]
            o += cols
        lin0, w1_0, w2_0, w1_1, w2_1 = (w[name] for name in ("lin0", "w1_0", "w2_0", "w1_1", "w2_1"))
        self0, lin1s, lin1v, r0 = (w[name] for name in ("self0", "lin1s", "lin1v", "r0"))
        l2t, l3 = w["l2t"][0:96], w["l3"][0:96]
        front = WEIGHTS["lin0"]
        r1 = sb("r1", [P, R1_COLS])
        edge_in = sb("edge_in", [P, ITER])
        hidden = sb("hidden", [P, ITER])
        idx = sb("idx", [P, 2, 2 * Q], I32)
        prod = sb("prod", [P, Q, 2, L0.pn])
        rows = sb("rows", [P, Q, 2, D])
        hot = sb("hot", [P, 2, 4, WIN])
        whot = sb("whot", [P, 2, 4, WIN, 4])
        stage = sb("stage", [P, 3, U0 * P])
        xs = sb("xs", [S, NB, P])[:]
        xv = sb("xv", [96, NB, P])[:]
        xs_flat, xv_flat = (a.rearrange("p t n -> p (t n)") for a in (xs, xv))
        x_rows = sb("x_rows", [P, NB, D])[:]
        pre = sb("pre", [P, NB, 192])[:]
        scratch = pre[:, :, 0:D]
        z_all = sb("z", [P, NB * D])[:]
        z = z_all.rearrange("p (t c) -> p t c", t=NB)
        zz = prod[:].rearrange("p q h c -> p (q h c)")[:, 0:NB * 2 * D].rearrange("p (t c) -> p t c", t=NB)
        zz_s = zz[:, :, 0:2 * S].rearrange("p t (m c) -> p t m c", m=2)
        zz_v = zz[:, :, 2 * S:2 * D].rearrange("p t (m c) -> p t m c", m=2)
        ts = sb("ts", [P, NB, P])[:]
        tv = sb("tv", [96, NB, 2, P])[:]
        h_out = sb("h_out", [P, NB, D])[:]
        base = sb("base", [P, NB, D])[:]
        gates = sb("gates", [P, NB, 96])
        coef = sb("coef", [P, n_steps, 3, NB])
        am = sb("am", [P, n_steps, 2, NB])
        stat = sb("stat", [P, 3, NB])
        eps = sb("eps", [P, 1])

        ps = ctx.enter_context(nc.psum_tensor("ps", [P, 8 * 512], F32))
        bank = [ps[:, 512 * b:512 * b + 512] for b in range(8)]
        hid_ps = ps[:, 0:2 * 512]
        windows = ps[:, 4 * 512:6 * 512]
        pre_ps = ps[:, 0:NB * 256].rearrange("p (t c) -> p t c", t=NB)
        n0_ps = [ps[:, 512 * b:512 * b + NB * 256].rearrange("p (t c) -> p t c", t=NB)[:, :, 0:D] for b in (0, 3)]
        far_turn_ps, flag_ps = bank[6][0:1, 0:P], bank[6][:, 320:321]
        comp_ps = bank[6][0:96, P:P + 192]
        turned = ps[:, 3 * 512:3 * 512 + NB * 3 * P].rearrange("p (t k c) -> p t k c", t=NB, k=3)
        LIN_BANKS = (7, 0, 1, 2, 7)

        h_dram = [nc.dram_tensor(f"h{l}_rows", [n_pad, D], F32).ap() for l in range(2)]
        base_dram = nc.dram_tensor("base_rows", [n_pad, D], F32).ap()

        loaded = sem("loaded")
        front_landed = sem("front_landed")
        front_scaled = sem("front_scaled")
        weights_landed = sem("weights_landed")
        weights_scaled = sem("weights_scaled")
        first_cast = sem("first_cast")
        first_spread = sem("first_spread")
        setup_step = sem("setup_step")
        far_found = sem("far_found")
        far_turned = sem("far_turned")
        flag_ready = sem("flag_ready")
        flag_spread = sem("flag_spread")
        r1_cleared = sem("r1_cleared")
        comp_ready = sem("comp_ready")
        comp_scaled = sem("comp_scaled")
        comp_placed = sem("comp_placed")
        acc_zeroed = sem("acc_zeroed")
        banks_cleared = sem("banks_cleared")
        edges_done = [sem(f"edges_done{l}") for l in range(2)]
        n0_in = [sem(f"n0_in{p}") for p in range(2)]
        n0_mm = sem("n0_mm")
        n0_out = sem("n0_out")
        n0_stored = sem("n0_stored")
        n1_in = sem("n1_in")
        n1_x_rows = sem("n1_x_rows")
        n1_staged = sem("n1_staged")
        n1_staged_pool = sem("n1_staged_pool")
        n1_tile = sem("n1_tile")
        n1_scaled = sem("n1_scaled")
        n1_gates = sem("n1_gates")
        n1_x1 = sem("n1_x1")
        n1_turned = sem("n1_turned")
        n1_copied = sem("n1_copied")
        n1_lin = sem("n1_lin")
        n1_lin_used = sem("n1_lin_used")
        n1_stored = sem("n1_stored")
        n2_in = sem("n2_in")
        n2_staged = sem("n2_staged")
        n2_staged_pool = sem("n2_staged_pool")
        n2_tile = sem("n2_tile")
        n2_scaled = sem("n2_scaled")
        n2_summed = sem("n2_summed")
        n2_out = sem("n2_out")
        n2_stored = sem("n2_stored")
        var_ready = [sem("n1_var"), sem("n2_var")]
        std_ready = [sem("n1_std"), sem("n2_std")]
        chain = [sem("n1_chain"), sem("n2_chain")]

        passed = sem("passed")

        block = ctx.enter_context(nc.Block())

        def wait(eng, s, value):
            if not isinstance(value, int) or value > 0:
                eng.wait_ge(s, value)

        def hold(eng, s, value):
            if not isinstance(value, int) or value > 0:
                eng.wait_ge(s, value)
                eng.sem_inc(passed, 1)

        def looped2(eng, count, body):
            body(0, 0)
            if count > 1:
                with eng.Fori(1, count - 1, 2) as i:
                    body(i, 1)
                    body(i + 1, 0)

        def looped(eng, count, body, first=1):
            for i in range(first):
                body(i)
            if count > first:
                with eng.Fori(first, count) as i:
                    body(i)

        def spread(ap, axis, n):
            ap = ap.unsqueeze(axis)
            shape = list(ap.shape)
            shape[axis] = n
            return ap.to_broadcast(shape)

        signed = [(r0[r:r + V, c:c + V], sign * INV_SQRT(2)) for r, c, sign in cross_parts()]
        comp = z_all[0:96, 0:192]
        comp_parts = [
            (r1[0:64, R1S:R1S + 128], comp[0:64, 0:128]),
            (r1[64:96, R1S + 128:R1S + 256], comp[64:96, 0:128]),
            (r1[96:128, R1S + 256:R1S + 384], comp[64:96, 0:128]),
            (r1[0:32, R1S + 384:R1S + 512], comp[64:96, 0:128]),
            (r1[0:64, R1W:R1W + 64], comp[0:64, 128:192]),
        ]
        for k in range(3):
            for m in range(2):
                col = R1V + 96 * m + V * k
                comp_parts.append((r1[V + V * k:2 * V + V * k, col:col + V], comp[64:96, 128 + V * m:128 + V * m + V]))

        setup = prod[:].rearrange("p q h c -> p (q h c)")
        dst_i = setup[:, 0:n_tiles].bitcast(I32)
        dst_f = setup[:, n_tiles:2 * n_tiles]
        far = setup[:, 2 * n_tiles:3 * n_tiles]
        first_f = setup[0:1, 3 * n_tiles:3 * n_tiles + n_pairs]
        o = 3 * n_tiles + n_pairs
        far_max = setup[:, o:o + 1]
        far_row = setup[0:1, o + 1:o + 2]
        flag_f = setup[0:1, o + 2:o + 3]
        flag_all = setup[:, o + 3:o + 4]
        ones = setup[0:1, o + 4:o + 4 + P]
        assert n_pairs <= 512 and o + 4 + P <= Q * 2 * L0.pn
        first_bc = bank[7][:, 0:n_pairs]

        tables = [(dst_i, ins["dst"]), (first[0:1, :], ins["first"]), (iota[:], ins["iota"]),
                  (ident[:], ins["ident"]), (attr[:], ins["attr"]), (coef[:], ins["coef"])]
        c0 = INV_SQRT(64) * INV_SQRT(16)
        c1 = INV_SQRT(16)
        C_S, C_X = math.sin(math.pi / 8.0), math.cos(math.pi / 8.0)
        scaled = [
            (self0[0:S, 0:96], INV_SQRT(S)), (self0[0:96, 96:192], INV_SQRT(V)),
            (r0[:, 0:R0B], c0 * INV_SQRT(128)),
            (r0[:, R0B:R0C].rearrange("p (k m c) -> p k m c", k=3, m=2)[:, :, 0], c0 * INV_SQRT(96) * INV_SQRT(3)),
            (r0[:, R0B:R0C].rearrange("p (k m c) -> p k m c", k=3, m=2)[:, :, 1], c0 * INV_SQRT(128)),
            (r0[:, R0C:R0D], c0 * INV_SQRT(128)), (r0[:, R0D:R0D + 96], c0 * INV_SQRT(96)),
            (lin1s[:, S:2 * S], C_S), (lin1v[0:96, 96:192], C_S),
            (lin1v[0:96, 288:384], C_S),
        ]

        def at(ap, j):
            if isinstance(j, int):
                return ap[j]
            ap = ap[bass.ds(j, 1)]
            return ap.rearrange("o p c -> (o p) c" if len(ap.shape) == 3 else "o p t c -> (o p) t c")

        def step_rows(dram):
            return dram.rearrange("(j t p) c -> j p t c", t=NB, p=P)

        def coef_of(table, j, m):
            if isinstance(j, int):
                return table[:, j, m]
            return table[:, bass.ds(j, 1)].rearrange("p o m t -> p (o m) t")[:, m]

        x_slots = [(xs_flat, xv_flat), (ts[0:S].rearrange("p t n -> p (t n)"),
                                        tv.rearrange("p t m n -> p (t m n)")[:, 0:NB * P])]

        STAGE_SLOT = (0, 1, 2, 0, 1)
        USED = (1, 1, 4, 2, 2)
        POOL_TILE = 2

        def stage_tiles(eng, copy, layer, staged, used, j, tiles):
            U = layer.units
            for t in tiles:
                c = j * NB + t
                s = acc[:, c * (U * P):(c + 1) * (U * P)] if isinstance(c, int) else \
                    acc[:, bass.ds(c * (U * P), U * P)]
                hold(eng, used, c - USED[t])
                copy(stage[:, STAGE_SLOT[t], 0:U * P], s).then_inc(staged, 1)

        def wait_staged(pe, by_act, by_pool, j, t):
            if t == POOL_TILE:
                pe.wait_ge(by_pool, j + 1)
            else:
                pe.wait_ge(by_act, j * (NB - 1) + (t + 1 if t < POOL_TILE else t))

        def unit(layer, t, u):
            return stage[:, STAGE_SLOT[t], 0:layer.units * P].rearrange("p (n u) -> p n u", u=layer.units)[:, :, u]

        def norm(dve, l, j, link):
            link(dve.tensor_reduce(stat[:, 0], z, AX.X, ALU.add))
            link(dve.tensor_scalar(stat[:, 1], stat[:, 0], 1.0 / D, None, ALU.mult))
            link(dve.tensor_tensor(z, z, spread(stat[:, 1], 2, D), ALU.subtract))
            link(dve.tensor_tensor(scratch, z, z, ALU.mult))
            dve.tensor_reduce(stat[:, 2], scratch, AX.X, ALU.add).then_inc(var_ready[l], 1)
            dve.wait_ge(std_ready[l], j + 1)
            link(dve.reciprocal(stat[:, 0], stat[:, 1]))

        def deviation(act, l, j):
            act.wait_ge(var_ready[l], j + 1)
            act.activation(stat[:, 1], stat[:, 2], ACT.Sqrt, bias=eps[:], scale=1.0 / D).then_inc(std_ready[l], 1)

        class Link:

            def __init__(self, eng, s, start):
                self.eng, self.s, self.start, self.n = eng, s, start, 0

            def __call__(self, ins_):
                self.n += 1
                ins_.then_inc(self.s, 1)
                self.eng.wait_ge(self.s, self.start + self.n)

        class Edge:
            def __init__(self, n):
                self.loaded = sem(f"e{n}_loaded")
                self.mixed = sem(f"e{n}_mixed")
                self.hidden = sem(f"e{n}_hidden")
                self.weights = sem(f"e{n}_weights")
                self.index = [sem(f"e{n}_index{p}") for p in range(2)]
                self.rows = [sem(f"e{n}_rows{q}") for q in range(Q)]
                self.hot = sem(f"e{n}_hot")
                self.whot = sem(f"e{n}_whot")
                self.prod = sem(f"e{n}_prod")
                self.agg = sem(f"e{n}_agg")
                self.added = sem(f"e{n}_added")
                self.window = sem(f"e{n}_window")

        edge = [Edge(0), Edge(1)]
        edge_feats = [ins["edge64"], ins["edge10"]]

        def edge_loads(sp, l):
            e = edge[l]

            def nodes(i, par):
                sp.dma_start(idx[:, par], at(ins["src"], i)).then_inc(e.index[par], 16)

            def features(i):
                s = at(edge_feats[l], i)
                if l == 0:
                    sp.dma_start(edge_in[:, 0:512], s).then_inc(e.loaded, 16)
                else:
                    sp.dma_start(edge_in[0:10, 0:512], s[0]).then_inc(e.loaded, 16)
                    sp.dma_start(edge_in[32:42, 0:512], s[1]).then_inc(e.loaded, 16)

            def body(i, par):
                hold(sp, e.mixed, i)
                features(i)
                for q in range(Q):
                    hold(sp, e.rows[q], 32 * i)
                nodes(i + 1, par)

            nodes(0, 0)
            nodes(1, 1)
            features(0)
            body(1, 0)
            with sp.Fori(2, n_iter - 2, 2) as i:
                body(i, 1)
                body(i + 1, 0)
            hold(sp, e.mixed, n_iter - 1)
            features(n_iter - 1)

        def edge_gathers(pool, l):
            e = edge[l]

            def body(i, par):
                hold(pool, e.index[par], 8 * i + 16 - 8 * par)
                for q in range(Q):
                    hold(pool, e.prod, i * Q + q - Q + 1)
                    for h in range(2):
                        pool.indirect_dma_start(
                            out=rows[:, q, h], out_offset=None, in_=h_dram[l],
                            in_offset=bass.IndirectOffsetOnAxis(ap=idx[:, par, 2 * q + h:2 * q + h + 1], axis=0),
                        ).then_inc(e.rows[q], 16)

            looped2(pool, n_iter, body)

        def edge_silu(act, l):
            e = edge[l]
            wide = P if l == 0 else GROUP
            scale = INV_SQRT(64) if l == 0 else 1.0

            def body(i):
                act.wait_ge(e.mixed, i + 1)
                for q in range(Q):
                    wait(act, e.weights, (i - 1) * Q + q + 1)
                    act.activation(hidden[:, q * wide:(q + 1) * wide], hid_ps[:, q * wide:(q + 1) * wide], ACT.Silu,
                                   scale=scale).then_inc(e.hidden, 1)

            looped(act, n_iter, body)

        def weights_of(q):
            b = 2 + 4 * (q % 2)
            return ps[:, 512 * b:512 * b + 1024].rearrange("p (h c) -> p h c", h=2)

        def edge_tensor(pe, l, layer, general):
            e = edge[l]
            lag = 0 if general else 2
            loads = 16 if l == 0 else 32

            def mix(i):
                pe.wait_ge(e.loaded, loads * i + loads)
                wait(pe, e.hidden, Q * i)
                if l == 0:
                    pe.matmul(bank[0], w1_0[:], edge_in[:, 0:512], start=True, stop=True).then_inc(e.mixed, 1)
                else:
                    pe.matmul(bank[0], w1_1[0:10], edge_in[0:10, 0:512], start=True, stop=True)
                    pe.matmul(bank[1], w1_1[32:42], edge_in[32:42, 0:512], start=True,
                              stop=True).then_inc(e.mixed, 1)

            def radial(i, q):
                pe.wait_ge(e.hidden, i * Q + q + 1)
                wait(pe, e.prod, i * Q + q - 1)
                w = weights_of(q)
                for h in range(2):
                    if l == 0:
                        r = slice(64 * h, 64 * h + 64)
                        mm = pe.matmul(w[:, h, 0:layer.wn], hidden[r, q * P:(q + 1) * P], w2_0[r], start=True,
                                       stop=True)
                    else:
                        c = (2 * q + h) * P
                        mm = pe.matmul(w[:, h, 0:layer.wn], hidden[:, c:c + P], w2_1[:], start=True, stop=True)
                mm.then_inc(e.weights, 1)

            def sums(q, slot):
                o = bank[4 + slot][:, 0:WIN * layer.units].rearrange("p (n u) -> p n u", u=layer.units)
                for h in range(2):
                    t = 2 * (q % 2) + h
                    for m, (c, size, attrs, u) in enumerate(layer.chunks):
                        count = len(range(4)[attrs])
                        mm = pe.matmul(o[0:size, :, u:u + count], prod[:, q, h, c:c + size],
                                       whot[:, slot, t, :, attrs], start=(t == 0 and m == 0),
                                       stop=(t == 3 and m == len(layer.chunks) - 1), skip_group_check=True)
                mm.then_inc(e.agg, 1)

            def lagged(i, q):
                n = i * Q + q - lag
                if isinstance(n, int) and n < 0:
                    return
                m = (q - lag) % Q
                if m % 2 == 0:
                    w = i * 2 + (q - lag) // 2
                    pe.wait_ge(e.whot, w + 1)
                    wait(pe, e.added, w - 1)
                pe.wait_ge(e.prod, n + 1)
                sums(m, m // 2)

            def body(i, last=False):
                for q in range(Q):
                    radial(i, q)
                    if q == 1 and not last:
                        mix(i + 1)
                    if not general:
                        lagged(i, q)
                    elif q % 2 == 1:
                        w = i * 2 + q // 2
                        hold(pe, e.prod, i * Q + q + 1)
                        with pe.Fori(0, n_win) as v:
                            pe.wait_ge(e.whot, w * n_win + v + 1)
                            sums(q - 1, 0)
                            sums(q, 0)

            pe.wait_ge(banks_cleared, l + 1)
            mix(0)
            looped(pe, n_iter - 1, body, first=2)
            body(n_iter - 1, last=True)
            if not general:
                for q in range(lag):
                    lagged(n_iter, q)

        def edge_vector(dve, l, layer, general):
            e = edge[l]
            U = layer.units

            def weighted_hot(w, slot, hot_slot, count, nodes):
                r = rel[:, w] if isinstance(w, int) else rel[:, bass.ds(w, 1)].rearrange("p o t -> p (o t)")
                dve.tensor_tensor(hot[:, hot_slot], spread(nodes, 1, 4), spread(r, 2, WIN),
                                  ALU.is_equal).then_inc(e.hot, 1)
                dve.wait_ge(e.hot, count + 1)
                a = attr[:, 4 * w:4 * w + 4] if isinstance(w, int) else attr[:, bass.ds(w * 4, 4)]
                dve.tensor_tensor(whot[:, slot], spread(hot[:, hot_slot], 3, 4), spread(a, 2, WIN),
                                  ALU.mult).then_inc(e.whot, 1)

            def products(i, q):
                dve.wait_ge(e.rows[q], 32 * i + 32)
                dve.wait_ge(e.weights, i * Q + q + 1)
                w = weights_of(q)
                dve.tensor_tensor(prod[:, q, :, 0:2 * S].rearrange("p h (k c) -> p h k c", k=2),
                                  w[:, :, 0:2 * S].rearrange("p h (k c) -> p h k c", k=2),
                                  spread(rows[:, q, :, 0:S], 2, 2), ALU.mult)
                for h in range(2):
                    ins_ = dve.tensor_tensor(
                        prod[:, q, h, 2 * S:layer.pn].rearrange("p (k i c) -> p k i c", k=layer.k, i=3),
                        spread(w[:, h, 2 * S:layer.wn].rearrange("p (k c) -> p k c", k=layer.k), 2, 3),
                        spread(rows[:, q, h, S:D].rearrange("p (i c) -> p i c", i=3), 1, layer.k), ALU.mult)
                ins_.then_inc(e.prod, 1)

            def add(w, slot):
                s = first[0:1, w:w + 1] if isinstance(w, int) else first[0:1, bass.ds(w, 1)]
                offset = dve.value_load(s, min_val=0, max_val=n_nodes - 1) * U
                dve.wait_ge(e.agg, 2 * w + 2)
                wait(dve, e.added, w)
                a = acc[:, bass.ds(offset, WIN * U)]
                dve.tensor_tensor(a, a, bank[4 + slot][:, 0:WIN * U], ALU.add).then_inc(e.added, 1)

            def body(i):
                for slot in range(2):
                    w = i * 2 + slot
                    if not general:
                        wait(dve, e.agg, i * Q + 2 * slot - 2)
                        weighted_hot(w, slot, slot, w, iota[:])
                        products(i, 2 * slot)
                        if not isinstance(i, int) or i > 0:
                            add(w - 2, slot)
                        products(i, 2 * slot + 1)
                        continue
                    products(i, 2 * slot)
                    products(i, 2 * slot + 1)
                    dve.tensor_copy(window[:], iota[:]).then_inc(e.window, 1)
                    hold(dve, e.window, w * (n_win + 1) + 1)
                    with dve.Fori(0, n_win) as v:
                        count = w * n_win + v
                        weighted_hot(w, 0, 0, count, window[:])
                        dve.wait_ge(e.agg, count * 2 + 2)
                        a = acc[:, bass.ds(v * (WIN * U), WIN * U)]
                        dve.tensor_tensor(a, a, bank[4][:, 0:WIN * U], ALU.add).then_inc(e.added, 1)
                        dve.wait_ge(e.added, count + 1)
                        dve.tensor_scalar(window[:], window[:], float(WIN), None, ALU.add).then_inc(e.window, 1)
                        dve.wait_ge(e.window, w * (n_win + 1) + v + 2)

            looped(dve, n_iter, body, first=2)
            if not general:
                for slot in range(2):
                    add(n_pairs - 2 + slot, slot)
                dve.wait_ge(e.added, n_pairs)
            dve.sem_inc(edges_done[l], 1)

        LINKS1, LINKS2 = 9, 6

        @block.sync
        def _(sp):
            for tile, s in tables[:3]:
                sp.dma_start(tile, s).then_inc(loaded, 16)
            sp.dma_start(weights[:, 0:front], ins["weights"][:, 0:front]).then_inc(front_landed, 16)
            for tile, name in zip(x_slots[0], ("xs", "xv")):
                sp.dma_start(tile, ins[name][0]).then_inc(n0_in[0], 16)
            for tile, s in tables[3:]:
                sp.dma_start(tile, s).then_inc(loaded, 16)
            sp.dma_start(weights[:, front:], ins["weights"][:, front:]).then_inc(weights_landed, 16)

            def load0(j, par):
                for tile, name in zip(x_slots[par], ("xs", "xv")):
                    sp.dma_start(tile, at(ins[name], j)).then_inc(n0_in[par], 16)

            def store0(j):
                hold(sp, n0_out, j + 2)
                sp.dma_start(at(step_rows(h_dram[0]), j), h_out).then_inc(n0_stored, 16)

            def rows0(j, par):
                hold(sp, n0_mm, j + 1)
                load0(j + 2, par)
                store0(j)

            load0(1, 1)
            looped2(sp, n_steps - 2, rows0)
            store0(n_steps - 2)
            store0(n_steps - 1)
            edge_loads(sp, 0)

            def load1(j):
                sp.dma_start(xs_flat, at(ins["xs"], j)).then_inc(n1_in, 16)
                sp.dma_start(xv_flat, at(ins["xv"], j)).then_inc(n1_in, 16)

            def load_rows1(j):
                sp.dma_start(x_rows, at(step_rows(ins["x_rows"]), j)).then_inc(n1_x_rows, 16)

            def store1(j):
                hold(sp, n1_lin_used, NB * j + NB)
                sp.dma_start(at(step_rows(h_dram[1]), j), h_out).then_inc(n1_stored, 16)
                sp.dma_start(at(step_rows(base_dram), j), base).then_inc(n1_stored, 16)

            load1(0)
            load_rows1(0)
            hold(sp, n1_tile, NB)
            load1(1)
            hold(sp, n1_x1, 1)
            load_rows1(1)
            with sp.Fori(1, n_steps - 1) as j:
                hold(sp, n1_tile, NB * j + NB)
                load1(j + 1)
                store1(j - 1)
                hold(sp, n1_x1, j + 1)
                load_rows1(j + 1)
            store1(n_steps - 2)
            store1(n_steps - 1)
            edge_loads(sp, 1)
            sp.wait_ge(n1_stored, 32 * n_steps)

            def load2(j):
                sp.dma_start(x_rows, at(step_rows(base_dram), j)).then_inc(n2_in, 16)

            def store2(j):
                hold(sp, n2_out, 2 * j + 2)
                sp.dma_start(at(step_rows(out), j), h_out).then_inc(n2_stored, 16)

            load2(0)
            with sp.Fori(1, n_steps) as j:
                hold(sp, n2_summed, j)
                load2(j)
                store2(j - 1)
            store2(n_steps - 1)
            sp.wait_ge(n2_stored, 16 * n_steps)

        @block.gpsimd
        def _(pool):
            pool.memset(acc[:], 0.0).then_inc(acc_zeroed, 1)
            pool.wait_ge(n0_stored, 16 * n_steps)
            edge_gathers(pool, 0)
            pool.wait_ge(edges_done[0], 1)
            a, cols = 0, n_pad * U1
            for j in range(n_steps):
                stage_tiles(pool, pool.tensor_copy, L0, n1_staged_pool, n1_tile, j, [POOL_TILE])
                b = min((j + 1) * NB * P * U0, cols)
                if a < b:
                    pool.wait_ge(n1_staged_pool, j + 1)
                    pool.wait_ge(n1_staged, (NB - 1) * (j + 1))
                    pool.memset(acc[:, a:b], 0.0).then_inc(acc_zeroed, 1)
                a = max(a, b)
            pool.wait_ge(n1_stored, 32 * n_steps)
            edge_gathers(pool, 1)
            pool.wait_ge(edges_done[1], 1)
            looped(pool, n_steps, lambda j: stage_tiles(pool, pool.tensor_copy, L1, n2_staged_pool, n2_tile, j,
                                                        [POOL_TILE]))

        zero_parts = len([j for j in range(n_steps) if j * NB * P * U0 < n_pad * U1])

        @block.scalar
        def _(act):
            edge_silu(act, 0)
            act.wait_ge(r1_cleared, 1)
            act.wait_ge(comp_scaled, 3)
            for tile, s in comp_parts:
                act.dma_start(tile, s).then_inc(comp_placed, 16)

            def gate(j):
                act.wait_ge(n1_scaled, j + 1)
                act.activation(gates[:], pre[:, :, 0:96], ACT.Sigmoid).then_inc(n1_gates, 1)

            def turned_to_sbuf(j):
                act.wait_ge(n1_turned, j + 1)
                act.activation(ts, turned[:, :, 0], ACT.Copy).then_inc(n1_copied, 1)
                act.activation(tv, turned[0:96, :, 1:3], ACT.Copy).then_inc(n1_copied, 1)

            act.wait_ge(edges_done[0], 1)

            def copy(out_, in_):
                return act.activation(out_, in_, ACT.Copy)

            by_act = [t for t in range(NB) if t != POOL_TILE]
            stage_tiles(act, copy, L0, n1_staged, n1_tile, 0, by_act)
            gate(0)
            with act.Fori(1, n_steps) as j:
                stage_tiles(act, copy, L0, n1_staged, n1_tile, j, by_act)
                deviation(act, 0, j - 1)
                turned_to_sbuf(j - 1)
                gate(j)
            deviation(act, 0, n_steps - 1)
            turned_to_sbuf(n_steps - 1)
            edge_silu(act, 1)
            act.wait_ge(edges_done[1], 1)
            stage_tiles(act, copy, L1, n2_staged, n2_tile, 0, by_act)
            with act.Fori(1, n_steps) as j:
                stage_tiles(act, copy, L1, n2_staged, n2_tile, j, by_act)
                deviation(act, 1, j - 1)
            deviation(act, 1, n_steps - 1)

        def branched(eng, edges, l, layer):
            eng.wait_ge(flag_ready, 1)
            far_flag = eng.value_load(flag[0:1, 0:1], min_val=0, max_val=1)
            with eng.If(far_flag < 1):
                edges(eng, l, layer, False)
            with eng.Else():
                edges(eng, l, layer, True)

        @block.tensor
        def _(pe):
            pe.wait_ge(first_cast, 2)
            pe.matmul(first_bc, ones, first_f, start=True, stop=True).then_inc(first_spread, 1)
            pe.wait_ge(front_scaled, 2)

            def rows0(j, par):
                pe.wait_ge(n0_in[par], 16 * j + 32 - 16 * par)
                wait(pe, n0_out, j)
                s, v = (a.rearrange("p (t n) -> p t n", t=NB) for a in x_slots[par])
                for t in range(NB):
                    pe.matmul(n0_ps[par][:, t, 0:S], s[:, t], lin0[0:S, 0:S], start=True, stop=True)
                    mm = pe.matmul(n0_ps[par][:, t, S:D], v[:, t], lin0[0:96, 96:192], start=True, stop=True)
                mm.then_inc(n0_mm, 1)

            looped2(pe, n_steps, rows0)
            pe.wait_ge(weights_landed, 16)
            for m, (a, b, c) in enumerate(((0, S, 0), (0, S, 64), (S, 96, 128), (S, 96, 160))):
                mm = pe.matmul(comp_ps[:, c:c + b - a], l2t[:, 96 * m:96 * m + 96], l3[:, a:b], start=True,
                               stop=True)
            mm.then_inc(comp_ready, 1)
            pe.wait_ge(far_found, 1)
            pe.wait_ge(loaded, 16 * len(tables))
            pe.matmul(far_turn_ps, far_max, ident[:], start=True, stop=True).then_inc(far_turned, 1)
            pe.wait_ge(flag_ready, 1)
            pe.matmul(flag_ps, ones, flag_f, start=True, stop=True).then_inc(flag_spread, 1)
            pe.wait_ge(n0_out, n_steps + 1)
            pe.wait_ge(comp_scaled, 3)
            branched(pe, edge_tensor, 0, L0)
            pe.wait_ge(edges_done[0], 1)
            pe.wait_ge(weights_scaled, len(scaled) + len(signed))

            def tile_sums(j, tiles):
                for t in tiles:
                    o = pre_ps[:, t]
                    wait_staged(pe, n1_staged, n1_staged_pool, j, t)
                    pe.matmul(o[:, 0:96], xs[:, t], self0[0:S, 0:96], start=True, stop=False)
                    pe.matmul(o[:, 96:192], xv[:, t], self0[0:96, 96:192], start=False, stop=False,
                              skip_group_check=True)
                    for u in range(3):
                        pe.matmul(o[:, 96:192], unit(L0, t, u), r0[:, R0A + 96 * u:R0A + 96 * u + 96], start=False,
                                  stop=False, skip_group_check=True)
                    for u in range(3, 6):
                        b, n = R0B + 192 * (u - 3), 192 if u < 5 else 96
                        pe.matmul(o[:, 0:n], unit(L0, t, u), r0[:, b:b + n], start=False, stop=False,
                                  skip_group_check=True)
                    pe.matmul(o[:, 96:192], unit(L0, t, 6), r0[:, R0C:R0C + 96], start=False,
                              stop=True, skip_group_check=True)
                    pe.matmul(o[:, 0:96], unit(L0, t, 7), r0[:, R0D:R0D + 96], start=False,
                              stop=True).then_inc(n1_tile, 1)

            def turn(j):
                pe.wait_ge(n1_x1, j + 1)
                for t in range(NB):
                    pe.transpose(turned[0:96, t, 1], zz_v[:, t, 0], ident[:])
                    pe.transpose(turned[0:96, t, 2], zz_v[:, t, 1], ident[:])
                    mm = pe.transpose(turned[:, t, 0], zz[:, t, 0:2 * S], ident[:])
                mm.then_inc(n1_turned, 1)

            def linears(j, scaled):
                pe.wait_ge(n1_copied, 2 * j + 2)
                for t in range(NB):
                    if t == 1:
                        pe.wait_ge(n1_scaled, scaled)
                    if t == NB - 1:
                        pe.wait_ge(n1_lin_used, j * NB + 1)
                    o = bank[LIN_BANKS[t]][:, 0:2 * D].rearrange("p (m c) -> p m c", m=2)
                    pe.matmul(o[:, :, 0:S], ts[:, t], lin1s[:], start=True, stop=True)
                    pe.matmul(o[:, :, S:D], tv[:, t, 0], lin1v[0:96, 0:192], start=True, stop=False)
                    pe.matmul(o[:, :, S:D], tv[:, t, 1], lin1v[0:96, 192:384], start=False,
                              stop=True).then_inc(n1_lin, 1)
                pe.wait_ge(n1_lin_used, j * NB + NB)

            pe.wait_ge(n1_in, 32)
            tile_sums(0, range(NB))
            with pe.Fori(1, n_steps) as j:
                pe.wait_ge(n1_in, 32 * j + 32)
                pe.wait_ge(n1_scaled, j)
                tile_sums(j, range(NB - 1))
                turn(j - 1)
                tile_sums(j, range(NB - 1, NB))
                linears(j - 1, j + 1)
            turn(n_steps - 1)
            linears(n_steps - 1, n_steps)
            branched(pe, edge_tensor, 1, L1)
            pe.wait_ge(edges_done[1], 1)
            pe.wait_ge(comp_placed, 16 * len(comp_parts))

            def rows2(j):
                wait(pe, n2_scaled, 2 * j)
                for t in range(NB):
                    wait_staged(pe, n2_staged, n2_staged_pool, j, t)
                    o = bank[t][:, 0:2 * D].rearrange("p (m c) -> p m c", m=2)
                    for m, u in enumerate((5, 0, 1, 4)):
                        pe.matmul(o[:, :, 0:S], unit(L1, t, u), r1[:, R1S + 128 * m:R1S + 128 * m + 128],
                                  start=(m == 0), stop=(m == 3))
                    pe.matmul(o[:, :, S:D], unit(L1, t, 3), r1[:, R1V:R1V + 192], start=True, stop=False)
                    for k in range(3):
                        mm = pe.matmul(o[:, :, S + V * k:S + V * k + V], unit(L1, t, k), r1[:, R1W:R1W + 64],
                                       start=False, stop=(k == 2))
                    mm.then_inc(n2_tile, 1)

            looped(pe, n_steps, rows2)

        @block.vector
        def _(dve):
            dve.memset(r1[:], 0.0).then_inc(r1_cleared, 1)
            dve.memset(eps[:], EPS).then_inc(setup_step, 1)
            dve.memset(ones, 1.0).then_inc(first_cast, 1)
            dve.wait_ge(front_landed, 16)
            dve.tensor_scalar(lin0[0:S, 0:S], lin0[0:S, 0:S], INV_SQRT(S), None, ALU.mult).then_inc(front_scaled, 1)
            dve.tensor_scalar(lin0[0:96, 96:192], lin0[0:96, 96:192], INV_SQRT(V), None,
                              ALU.mult).then_inc(front_scaled, 1)
            dve.wait_ge(loaded, 16 * len(tables))
            link = Link(dve, setup_step, 1)
            dve.tensor_copy(first_f, first[0:1, :]).then_inc(first_cast, 1)
            link(dve.tensor_copy(dst_f, dst_i))
            for m in range(2):
                dve.tensor_tensor(am[:, :, m], coef[:, :, m], coef[:, :, 2], ALU.mult)
            dve.wait_ge(first_spread, 1)
            link(dve.tensor_tensor(rel[:], dst_f.rearrange("p (w t) -> p w t", t=4), spread(first_bc, 2, 4),
                                   ALU.subtract))
            middle = (WIN - 1) / 2
            link(dve.tensor_scalar(far, rel[:].rearrange("p w t -> p (w t)"), middle, None, ALU.subtract))
            link(dve.tensor_tensor(far, far, far, ALU.mult))
            dve.tensor_reduce(far_max, far, AX.X, ALU.max).then_inc(far_found, 1)
            dve.sem_inc(n0_out, 1)

            def rows0(j, par):
                dve.wait_ge(n0_mm, j + 1)
                wait(dve, n0_stored, 16 * j)
                dve.tensor_tensor(h_out, n0_ps[par], spread(coef_of(coef, j, 0), 2, D),
                                  ALU.mult).then_inc(n0_out, 1)

            looped2(dve, n_steps, rows0)
            dve.wait_ge(far_turned, 1)
            link(dve.tensor_reduce(far_row, far_turn_ps, AX.X, ALU.max))
            link(dve.tensor_scalar(flag_f, far_row, (middle + 0.5) ** 2, None, ALU.is_gt))
            dve.tensor_copy(flag[0:1, 0:1], flag_f).then_inc(flag_ready, 1)
            dve.wait_ge(flag_spread, 1)
            link(dve.tensor_copy(flag_all, flag_ps))
            link(dve.scalar_tensor_tensor(out=rel[:], in0=spread(first_bc, 2, 4), scalar=flag_all,
                                          in1=rel[:], op0=ALU.mult, op1=ALU.add))
            dve.wait_ge(comp_ready, 1)
            g = c1 * C_X
            dve.tensor_scalar(comp[0:64, :], comp_ps[0:64], g, None, ALU.mult).then_inc(comp_scaled, 1)
            dve.tensor_scalar(comp[64:96, 0:128], comp_ps[64:96, 0:128], g * INV_SQRT(3), None,
                              ALU.mult).then_inc(comp_scaled, 1)
            dve.tensor_scalar(comp[64:96, 128:192], comp_ps[64:96, 128:192], g, None,
                              ALU.mult).then_inc(comp_scaled, 1)
            dve.memset(windows, 0.0).then_inc(banks_cleared, 1)
            dve.wait_ge(weights_landed, 16)
            for tile, factor in scaled:
                dve.tensor_scalar(tile, tile, factor, None, ALU.mult).then_inc(weights_scaled, 1)
            dve.wait_ge(weights_scaled, len(scaled))
            for tile, factor in signed:
                dve.tensor_scalar(tile, tile, factor, None, ALU.mult).then_inc(weights_scaled, 1)
            dve.wait_ge(acc_zeroed, 1)
            branched(dve, edge_vector, 0, L0)

            def scale(j):
                dve.wait_ge(n1_tile, NB * j + NB)
                dve.tensor_tensor(pre, pre_ps[:, :, 0:192], spread(coef_of(coef, j, 0), 2, 192),
                                  ALU.mult).then_inc(n1_scaled, 1)

            def gated(j):
                link = Link(dve, chain[0], j * LINKS1)
                dve.wait_ge(n1_gates, j + 1)
                link(dve.tensor_tensor(z[:, :, 0:S], pre[:, :, 0:S], gates[:, :, 0:S], ALU.mult))
                link(dve.tensor_tensor(
                    z[:, :, S:D].rearrange("p t (i c) -> p t i c", i=3),
                    pre[:, :, 96:192].rearrange("p t (i c) -> p t i c", i=3),
                    spread(gates[:, :, S:96], 2, 3), ALU.mult))
                dve.wait_ge(n1_x_rows, 16 * j + 16)
                link(dve.tensor_tensor(z, z, x_rows, ALU.add))
                norm(dve, 0, j, link)
                link(dve.tensor_tensor(z, z, spread(stat[:, 0], 2, D), ALU.mult))
                ac = coef_of(coef, j, slice(0, 2)).rearrange("p m t -> p t m")
                dve.tensor_tensor(zz_s, spread(z[:, :, 0:S], 2, 2), spread(ac, 3, S), ALU.mult)
                dve.tensor_tensor(zz_v, spread(z[:, :, S:D], 2, 2), spread(ac, 3, D - S), ALU.mult).then_inc(n1_x1, 1)
                assert link.n == LINKS1, link.n

            def collect(j):
                for t in range(NB):
                    dve.wait_ge(n1_lin, j * NB + t + 1)
                    o = bank[LIN_BANKS[t]]
                    dve.tensor_copy(h_out[:, t], o[:, 0:D])
                    dve.tensor_tensor(base[:, t], o[:, D:2 * D], z[:, t], ALU.add).then_inc(n1_lin_used, 1)

            dve.wait_ge(comp_placed, 16 * len(comp_parts))
            scale(0)
            gated(0)
            with dve.Fori(1, n_steps) as j:
                scale(j)
                collect(j - 1)
                dve.wait_ge(n1_lin_used, NB * j)
                gated(j)
                dve.wait_ge(n1_stored, 32 * j)
            collect(n_steps - 1)
            dve.wait_ge(acc_zeroed, 1 + zero_parts)
            dve.memset(windows, 0.0).then_inc(banks_cleared, 1)
            branched(dve, edge_vector, 1, L1)

            def rows2(j):
                link = Link(dve, chain[1], j * LINKS2)
                dve.wait_ge(n2_tile, NB * j + NB)
                wait(dve, n2_out, 2 * j)
                o = ps[:, 0:NB * 512].rearrange("p (t c) -> p t c", t=NB)
                dve.tensor_tensor(z, o[:, :, 0:D], spread(coef_of(am, j, 0), 2, D), ALU.mult).then_inc(n2_scaled, 1)
                dve.tensor_tensor(scratch, o[:, :, D:2 * D], spread(coef_of(am, j, 1), 2, D),
                                  ALU.mult).then_inc(n2_scaled, 1)
                dve.wait_ge(n2_scaled, 2 * j + 2)
                link(dve.tensor_tensor(z, z, scratch, ALU.add))
                dve.wait_ge(n2_in, 16 * j + 16)
                dve.tensor_tensor(z, z, x_rows, ALU.add).then_inc(n2_summed, 1)
                dve.wait_ge(n2_summed, j + 1)
                norm(dve, 1, j, link)
                wait(dve, n2_stored, 16 * j)
                dve.tensor_tensor(h_out[:, :, 0:S], z[:, :, 0:S], spread(stat[:, 0], 2, S),
                                  ALU.mult).then_inc(n2_out, 1)
                dve.tensor_tensor(h_out[:, :, S:D].rearrange("p t (c i) -> p t i c", i=3),
                                  z[:, :, S:D].rearrange("p t (i c) -> p t i c", i=3),
                                  spread(spread(stat[:, 0], 2, 3), 3, V), ALU.mult).then_inc(n2_out, 1)
                assert link.n == LINKS2, link.n

            looped(dve, n_steps, rows2)


def placed_weights(given):
    import numpy as np
    tiles = {name: np.zeros((P, cols), np.float32) for name, cols in WEIGHTS.items()}

    def put(name, row, col, block):
        tiles[name][row:row + block.shape[0], col:col + block.shape[1]] = block

    g0 = {name[len("L0_gnn_"):]: np.asarray(a) for name, a in given.items() if name.startswith("L0_gnn_")}
    g1 = {name[len("L1_gnn_"):]: np.asarray(a) for name, a in given.items() if name.startswith("L1_gnn_")}
    for h in range(2):
        put("w1_0", S * h, S * h, g0["fc_w1"])
        put("w1_1", 32 * h, 0, g1["W_fc1"])
        for col, a, b in ((0, 0, 128), (128, 192, 224), (160, 160, 192), (192, 128, 160)):
            put("w2_0", S * h, col, g0["fc_w2"][:, a:b])
    for col, a, b in ((0, 0, 128), (128, 160, 192), (160, 128, 160)):
        put("w2_1", 0, col, g1["W_fc2"][:, a:b])
    put("lin0", 0, 0, g0["lin1_ws"])
    put("self0", 0, 0, g0["sc_ws"])
    for i in range(3):
        put("lin0", V * i, 96 + V * i, g0["lin1_wv"])
        put("self0", V * i, 96 + V * i, g0["sc_wv"])
    for m, part in enumerate(("l1_a", "sc_a", "l1_c", "sc_c")):
        put("lin1s", S * (m // 2), S * (m % 2), g1[f"Ws_{part}"])
        for i in range(3):
            put("lin1v", V * i, 96 * m + V * i, g1[f"Wv_{part}"])
    lin2s, lin2v = g0["lin2_ws"], g0["lin2_wv"]
    put("r0", 0, R0D, lin2s[0:64])
    for k in range(3):
        put("r0", 0, R0A + 96 * k + V * k, lin2v[0:64])
        put("r0", V + V * k, R0B + 192 * k, lin2s[64:96])
        put("r0", V * k, R0C + V * k, lin2v[64:96])
    for row, col, _ in cross_parts():
        put("r0", row, col, lin2v[96:128])
    for m, part in enumerate(("Ws_l2_a", "Ws_l2_c", "Wv_l2_a", "Wv_l2_c")):
        put("l2t", 0, 96 * m, g1[part].T)
    put("l3", 0, 0, g1["Ws_l3"])
    put("l3", 0, S, g1["Wv_l3"])
    return np.concatenate(list(tiles.values()), 1)


def kernel(x, src, dst, edge_attr_10, edge_attr_4, edge_attr_64, node_vec1, node_vec1_n2, node_vec1_n3, **weights):
    import numpy as np
    import concourse.bacc as bacc
    from concourse.bass_utils import run_bass_kernel_spmd

    x, src, dst = np.asarray(x), np.asarray(src), np.asarray(dst)
    n, e = x.shape[0], src.shape[0]
    n_iter = iterations(e)
    e_pad = n_iter * ITER
    n_steps = node_steps(n)
    n_pad = n_steps * NB * P

    def pad(a, rows, **kw):
        a = np.asarray(a)
        return np.pad(a, [(0, rows - a.shape[0])] + [(0, 0)] * (a.ndim - 1), **kw)

    def by_tile(a):
        return np.ascontiguousarray(np.moveaxis(a.reshape(-1, TILE, *a.shape[1:]), 0, 1))

    xp = pad(x, n_pad)
    x_rows = np.concatenate([xp[:, :S], xp[:, S:].reshape(n_pad, V, 3).transpose(0, 2, 1).reshape(n_pad, 3 * V)], 1)
    turned = x_rows.reshape(n_steps, NB * P, D).transpose(0, 2, 1)
    coef = np.concatenate([pad(a, n_pad) for a in (node_vec1, node_vec1_n2, node_vec1_n3)], 1)
    dst_p = pad(dst, e_pad, mode="edge")
    e64 = pad(edge_attr_64, e_pad).reshape(n_iter, Q, 2, TILE, 64)
    arrays = {
        "x_rows": x_rows,
        "xs": turned[:, :S], "xv": turned[:, S:],
        "coef": coef.reshape(n_steps, NB, P, 3).transpose(2, 0, 3, 1),
        "src": pad(src, e_pad).reshape(n_iter, 2 * Q, TILE).transpose(0, 2, 1),
        "dst": by_tile(dst_p), "first": dst_p[::PAIR][None],
        "attr": by_tile(pad(edge_attr_4, e_pad)),
        "edge64": e64.transpose(0, 2, 4, 1, 3).reshape(n_iter, P, ITER // 2),
        "edge10": pad(edge_attr_10, e_pad).reshape(n_iter, 2, ITER // 2, 10).transpose(0, 1, 3, 2),
        "iota": np.tile(np.arange(WIN, dtype=np.float32), (P, 1)),
        "ident": np.eye(P, dtype=np.float32),
    }
    arrays["weights"] = placed_weights(weights)

    nc = bacc.Bacc("TRN2", target_bir_lowering=False, num_devices=1)
    arrays = {k: np.ascontiguousarray(a) for k, a in arrays.items()}
    ins = {k: nc.dram_tensor(f"in_{k}", a.shape, mybir.dt.from_np(a.dtype), kind="ExternalInput").ap()
           for k, a in arrays.items()}
    out = nc.dram_tensor("out", (n_pad, D), F32, kind="ExternalOutput").ap()
    gnn_kernel(nc, ins, out, n, e)
    r = run_bass_kernel_spmd(nc, [{f"in_{k}": a for k, a in arrays.items()}], core_ids=[0])
    return r.results[0]["out"][:n]
```
